# Optimizing a Trainium2 kernel written in Bass

```python
import numpy as np
import jax
import jax.numpy as jnp

def _softmax(x, axis=-1):
    return jax.nn.softmax(x, axis=axis)

def _gelu(x):
    return jax.nn.gelu(x, approximate=True)

def _silu(x):
    return jax.nn.silu(x)

def _sigmoid(x):
    return jax.nn.sigmoid(x)

def _layernorm(x, axis=-1, eps=1e-05):
    m = jnp.mean(x, axis=axis, keepdims=True)
    v = jnp.var(x, axis=axis, keepdims=True)
    return (x - m) / jnp.sqrt(v + eps)

def _scatter_add(tgt, idx, src, axis=0):
    return tgt.at[idx].add(src)

def _segment_sum(src, seg, n):
    return jax.ops.segment_sum(src, seg, n)
kernel_name = 'mk_flamingo_gated_d1_seqx_r4_5454b6'

def setup_inputs(seed: int=0):
    np.random.seed(seed)
    _w = jnp.asarray

    def _rec_inputs():
        import jax
        import jax.numpy as jnp
        _rk = jax.random.key(seed)
        x = 7.22e-05 + 1 * jax.random.normal(jax.random.fold_in(_rk, 1), (16, 128, 512), jnp.float32)
        _lenS = 128 - jax.random.randint(jax.random.fold_in(_rk, 7), (16,), 0, max(1, 128 // 4) + 1, jnp.int32)
        _lenS2 = 128 - jax.random.randint(jax.random.fold_in(_rk, 8), (16,), 0, max(1, 128 // 4) + 1, jnp.int32)
        _ctx_512P = jax.random.normal(jax.random.fold_in(_rk, 11), (16, 16, 128), jnp.float32)
        _ctx_512c = jax.random.dirichlet(jax.random.fold_in(_rk, 511), 0.3 * jnp.ones((16,), jnp.float32), (16, 128))
        _ctx_512t = jnp.einsum('bsk,bkd->bsd', _ctx_512c, _ctx_512P)
        _ctx_512t = _ctx_512t * jax.lax.rsqrt(jnp.mean(jnp.square(_ctx_512t)) + 1e-12) * 0.953939
        ctx_512 = -0.000514642 + 1.00011 * (_ctx_512t + 0.3 * jax.random.normal(jax.random.fold_in(_rk, 611), (16, 128, 128), jnp.float32))
        _g = jax.random.normal(jax.random.fold_in(_rk, 9001), (2, 1), jnp.float32)
        _g = jnp.sign(_g) * jnp.maximum(jnp.abs(_g), 1.0) + (_g == 0) * 1.0
        g_xattn = _g[0]
        g_ffn = _g[1]
        return (x, ctx_512, g_xattn, g_ffn)
    x, ctx_512, g_xattn, g_ffn = _rec_inputs()

    def _L0_xattn_setup():
        import jax, jax.numpy as jnp
        import numpy as np
        import math
        D_MODEL = 512
        N_HEADS = 16
        N_GROUPS = 4
        HEADS_PER_GROUP = N_HEADS // N_GROUPS
        HEAD_DIM = D_MODEL // N_HEADS
        B, S = (2, 512)
        key = jax.random.key(seed)
        k1, k2, k3, k4, k5 = jax.random.split(key, 5)
        q = jax.random.normal(k1, (B, S, D_MODEL), dtype=jnp.float32)
        k = jax.random.normal(k2, (B, S, N_GROUPS * HEAD_DIM), dtype=jnp.float32)
        v = jax.random.normal(k3, (B, S, N_GROUPS * HEAD_DIM), dtype=jnp.float32)
        lim = 1.0 / math.sqrt(D_MODEL)
        Wc = jax.random.uniform(k4, (D_MODEL, D_MODEL), minval=-lim, maxval=lim, dtype=jnp.float32)
        bc = jax.random.uniform(k5, (D_MODEL,), minval=-lim, maxval=lim, dtype=jnp.float32)
        return {'q': q, 'k': k, 'v': v, 'Wc': Wc, 'bc': bc}
    _L0_xattn_all = _L0_xattn_setup()
    _L0_xattn_in = {k: v for k, v in _L0_xattn_all.items() if k in ('Wc', 'bc')}
    del _L0_xattn_all

    def _L0_ffn_setup():
        import jax, jax.numpy as jnp
        import numpy as np
        H = 512
        E = 16
        I = 128
        IS = 512
        TOP_K = 2
        B, S = (1, 512)
        key = jax.random.key(seed)
        ks = jax.random.split(key, 9)
        std = 0.02
        return {'hidden_states': jax.random.normal(ks[0], (B, S, H), dtype=jnp.float32), 'gate_w': jax.random.normal(ks[1], (E, H), dtype=jnp.float32) * std, 'w1': jax.random.normal(ks[2], (E, I, H), dtype=jnp.float32) * std, 'w2': jax.random.normal(ks[3], (E, H, I), dtype=jnp.float32) * std, 'w3': jax.random.normal(ks[4], (E, I, H), dtype=jnp.float32) * std, 'ws_gate': jax.random.normal(ks[5], (IS, H), dtype=jnp.float32) * std, 'ws_up': jax.random.normal(ks[6], (IS, H), dtype=jnp.float32) * std, 'ws_down': jax.random.normal(ks[7], (H, IS), dtype=jnp.float32) * std, 'shared_gate_w': jax.random.normal(ks[8], (1, H), dtype=jnp.float32) * std}
    _L0_ffn_all = _L0_ffn_setup()
    _L0_ffn_in = {k: v for k, v in _L0_ffn_all.items() if k in ('gate_w', 'w1', 'w2', 'w3', 'ws_gate', 'ws_up', 'ws_down', 'shared_gate_w')}
    del _L0_ffn_all
    return {'x': x, 'ctx_512': ctx_512, 'g_xattn': g_xattn, 'g_ffn': g_ffn, 'L0_xattn_Wc': _L0_xattn_in['Wc'], 'L0_xattn_bc': _L0_xattn_in['bc'], 'L0_ffn_gate_w': _L0_ffn_in['gate_w'], 'L0_ffn_w1': _L0_ffn_in['w1'], 'L0_ffn_w2': _L0_ffn_in['w2'], 'L0_ffn_w3': _L0_ffn_in['w3'], 'L0_ffn_ws_gate': _L0_ffn_in['ws_gate'], 'L0_ffn_ws_up': _L0_ffn_in['ws_up'], 'L0_ffn_ws_down': _L0_ffn_in['ws_down'], 'L0_ffn_shared_gate_w': _L0_ffn_in['shared_gate_w']}

def reference(x, ctx_512, g_xattn, g_ffn, L0_xattn_Wc, L0_xattn_bc, L0_ffn_gate_w, L0_ffn_w1, L0_ffn_w2, L0_ffn_w3, L0_ffn_ws_gate, L0_ffn_ws_up, L0_ffn_ws_down, L0_ffn_shared_gate_w):
    import jax
    import jax.numpy as jnp

    def _L0_xattn_ref(q, k, v, Wc, bc):
        import jax, jax.numpy as jnp
        import numpy as np
        import math
        D_MODEL = 512
        N_HEADS = 16
        N_GROUPS = 4
        HEADS_PER_GROUP = N_HEADS // N_GROUPS
        HEAD_DIM = D_MODEL // N_HEADS
        B, S = (2, 512)
        b, s, _ = q.shape
        qh = q.reshape(b, s, N_GROUPS, HEADS_PER_GROUP, HEAD_DIM).transpose(0, 2, 3, 1, 4)
        kh = k.reshape(b, s, N_GROUPS, HEAD_DIM).transpose(0, 2, 1, 3)
        vh = v.reshape(b, s, N_GROUPS, HEAD_DIM).transpose(0, 2, 1, 3)
        scale = 1.0 / math.sqrt(HEAD_DIM)
        scores = jnp.einsum('bghsd,bgtd->bghst', qh, kh) * scale
        probs = jax.nn.softmax(scores, axis=-1)
        out = jnp.einsum('bghst,bgtd->bghsd', probs, vh)
        out = out.transpose(0, 3, 1, 2, 4).reshape(b, s, D_MODEL)
        return out @ Wc.T + bc

    def _L0_ffn_ref(hidden_states, gate_w, w1, w2, w3, ws_gate, ws_up, ws_down, shared_gate_w):
        import jax, jax.numpy as jnp
        import numpy as np
        H = 512
        E = 16
        I = 128
        IS = 512
        TOP_K = 2
        B, S = (1, 512)
        b, s, h = hidden_states.shape
        x = hidden_states.reshape(-1, h)
        T = x.shape[0]
        router_logits = x @ gate_w.T
        routing = jax.nn.softmax(router_logits.astype(jnp.float32), axis=-1)
        topw, sel = jax.lax.top_k(routing, TOP_K)
        topw = topw / jnp.sum(topw, axis=-1, keepdims=True)
        topw = topw.astype(x.dtype)
        combine = jnp.zeros((T, E), dtype=x.dtype).at[jnp.arange(T)[:, None], sel].set(topw)
        hmid = jax.nn.silu(jnp.einsum('th,eih->tei', x, w1)) * jnp.einsum('th,eih->tei', x, w3)
        hmid = hmid * combine[:, :, None]
        moe_out = jnp.einsum('tei,ehi->th', hmid, w2)
        shared = jax.nn.silu(x @ ws_gate.T) * (x @ ws_up.T) @ ws_down.T
        shared = jax.nn.sigmoid(x @ shared_gate_w.T) * shared
        return (moe_out + shared).reshape(b, s, h)
    x = x + jnp.tanh(g_xattn[0]) * _L0_xattn_ref(_layernorm(x, axis=-1), ctx_512, ctx_512, L0_xattn_Wc, L0_xattn_bc)
    x = x + jnp.tanh(g_ffn[0]) * _L0_ffn_ref(_layernorm(x, axis=-1), L0_ffn_gate_w, L0_ffn_w1, L0_ffn_w2, L0_ffn_w3, L0_ffn_ws_gate, L0_ffn_ws_up, L0_ffn_ws_down, L0_ffn_shared_gate_w)
    return x

_drawn_inputs = setup_inputs


def setup_inputs(seed=0):
    import zlib

    import numpy as np

    out = dict(_drawn_inputs(seed))
    spreads = {}
    factors = {'L0_xattn_bc': 3.05,
     'L0_ffn_gate_w': 3.74,
     'L0_ffn_w1': 3.57,
     'L0_ffn_w2': 3.508,
     'L0_ffn_w3': 3.514,
     'L0_ffn_shared_gate_w': 35.377,
     'L0_ffn_ws_gate': 2.763,
     'L0_ffn_ws_up': 2.729,
     'L0_ffn_ws_down': 2.717}
    for name, (base, spread) in spreads.items():
        noise = np.random.default_rng([zlib.crc32(name.encode()), seed]).standard_normal(out[name].shape)
        drawn = base * np.exp(spread * noise) if base else spread * noise
        out[name] = jnp.asarray(drawn.astype(out[name].dtype))
    for name, factor in factors.items():
        out[name] = (out[name] * factor).astype(out[name].dtype)
    return out
```

```python
from contextlib import ExitStack

import concourse.bass as bass
from concourse import mybir

F32 = mybir.dt.float32
BF16 = mybir.dt.bfloat16
I32 = mybir.dt.int32
U32 = mybir.dt.uint32
ALU = mybir.AluOpType
ACT = mybir.ActivationFunctionType
AX = mybir.AxisListType

P = 128
B = 16
D = 512
DC = D // P
NG = 4
HG = 4
HD = 32
H = NG * HG
E = 16
I = 128
IS = 512
IC = IS // P
TOPK = 2
NT = B * P * TOPK // P + E - 1
EPS = 1e-5
MACRO = 512
NM = B * P // MACRO
TM = MACRO // P
LAG = 3
RING = 4
FLOOR = 0.5 - 0.5 / P


def need(eng, sem, value):
    if isinstance(value, int) and value <= 0:
        return
    eng.wait_ge(sem, value)


def flamingo_block(nc, x, ctx, g_xattn, g_ffn, wc_t, bc, gate_t, sgate_t, w13_t, w2_t, wsg_t, wsu_t, wsd_t,
                   xn_dram, y_dram, table_dram, out):
    x_tiles = x.rearrange("(b p) d -> b p d", p=P)
    ctx_tiles = ctx.rearrange("(b p) d -> b p d", p=P)
    xn_tiles = xn_dram.rearrange("(b p) d -> b p d", p=P)
    out_tiles = out.rearrange("(b p) d -> b p d", p=P)
    y_slots = y_dram.rearrange("(p t) d -> t p d", t=NT)
    table_slots = table_dram.rearrange("(p t) o -> p (t o)", t=NT)

    with ExitStack() as stack:
        def sb(name, shape, dt=F32):
            return stack.enter_context(nc.sbuf_tensor(name, shape, dt))

        def sem(name):
            return stack.enter_context(nc.semaphore(name))

        xs = sb("xs", [P, B, D])
        xnT = sb("xnT", [P, DC, B * P])
        experts = sb("experts", [P, E * (DC * 2 * I + D)])
        w13 = experts[:, 0:E * DC * 2 * I].rearrange("p (ec n) -> p ec n", n=2 * I)
        w2 = experts[:, E * DC * 2 * I:E * (DC * 2 * I + D)].rearrange("p (e n) -> p e n", n=D)
        ws_gate = sb("ws_gate", [P, DC, IS])
        ws_up = sb("ws_up", [P, DC, IS])
        ws_down = sb("ws_down", [P, IC, D])
        shared = sb("shared", [P, 4 * D])
        wc = shared[:, :].rearrange("p (j n) -> p j n", j=HG)
        gates = sb("gates", [P, DC, E + 1])
        ident = sb("ident", [P, P])
        strict_upper = sb("strict_upper", [P, P], BF16)
        ones_bf = sb("ones_bf", [P, P], BF16)
        tanh_g = sb("tanh_g", [P, 2])
        minus_half = sb("minus_half", [P, 1])
        weight = sb("weight", [P, 3, B])
        slot_row = sb("slot_row", [P, TOPK, B], I32)
        token_id = sb("token_id", [P, B], I32)
        slot_token = sb("slot_token", [P, NT], I32)
        tokens_now = sb("tokens_now", [P, RING], I32)
        tile_expert = sb("tile_expert", [P, NT], I32)
        gathered = sb("gathered", [P, RING, D])
        silu_c = sb("silu_c", [P, 2, I])
        hid = sb("hid", [P, 2, I])
        hidT = sb("hidT", [P, 2, P])

        used = [0]

        def own(n, dt=F32):
            a = experts[:, used[0]:used[0] + n]
            used[0] += n
            return a if dt == F32 else a.bitcast(dt)

        qT = own(2 * D).rearrange("p (u n) -> p u n", u=2)
        ctxs = own(2 * P).rearrange("p (u n) -> p u n", u=2)
        ctx_rep = own(D)
        kT_rep = own(D)
        k_diag = own(NG * HG * P)
        v_pad = own(2 * NG * (P + HD)).rearrange("p (u g c) -> p u g c", u=2, g=NG)
        probs = own(H * P)
        probsT = own(NG * D).rearrange("p (g n) -> p g n", g=NG)
        oT = own(2 * D).rearrange("p (u n) -> p u n", u=2)
        xn = own(2 * D).rearrange("p (u n) -> p u n", u=2)
        xn2 = own(2 * D).rearrange("p (u n) -> p u n", u=2)
        bias_out = own(D)
        neg_max = own(H)
        row_sum = own(H)
        inv_sum = own(H)
        stats1, stats2 = own(6), own(6)
        mean1, mean2 = own(2), own(2)
        var1, var2 = own(1), own(1)
        rstd1, rstd2 = own(2), own(2)
        logitsT = own(B * P)
        logits = own(B * (E + 1)).rearrange("p (b e) -> p b e", b=B)
        top8 = own(B * 8).rearrange("p (b n) -> p b n", b=B)
        top8_at = own(B * 8, U32).rearrange("p (b n) -> p b n", b=B)
        expert_of = own(TOPK * B).rearrange("p (k b) -> p k b", k=TOPK)
        iota_e = own(E)
        iota_t = own(NT)
        tri_e = own(E * E)
        picked = own(TOPK * B * E).rearrange("p (k n) -> p k n", k=TOPK)
        picked_any = own(B * E // 2, BF16)
        count_e, tiles_e, start_e, end_e = own(E), own(E), own(E), own(E)
        tiles_int = own(E, I32)
        before = own(E * E)
        full_tiles = own(B * E)
        full_int = own(B * E, I32)
        place = own(B * E)
        place_k = own(TOPK * B * E).rearrange("p (k n) -> p k n", k=TOPK)
        row_f = own(TOPK * B).rearrange("p (k b) -> p k b", k=TOPK)
        passed = own(NT * E)
        expert_f = own(NT)
        zeros_i = own(NT, I32)
        gap = own(2 * B)
        assert used[0] <= E * (DC * 2 * I + D)
        silu_s = shared[:, 0:2 * MACRO].rearrange("p (u n) -> p u n", u=2)
        hidT_s = shared[:, 2 * MACRO:4 * MACRO].rearrange("p (u n) -> p u n", u=2)
        xgT = shared[:, 0:2 * D].rearrange("p (u n) -> p u n", u=2)
        y_sb = shared[:, 2 * D:4 * D].rearrange("p (u n) -> p u n", u=2)
        y_back = ws_gate[:, :, :].rearrange("p (n k) d -> p n k d", k=TOPK)

        bank = [stack.enter_context(nc.psum_tensor(f"bank{i}", [P, 512], F32)) for i in range(8)]
        turn = [bank[4], bank[5]]
        out_bank, wc_bank = bank[6], bank[7]

        loaded = sem("loaded")
        wc_loaded = sem("wc_loaded")
        shared_loaded = sem("shared_loaded")
        x_loaded = sem("x_loaded")
        ctx_loaded = sem("ctx_loaded")
        w13_loaded = sem("w13_loaded")
        w2_loaded = sem("w2_loaded")
        consts = sem("consts")
        consts_p = sem("consts_p")
        ident_zeroed = sem("ident_zeroed")
        gates_tanh = sem("gates_tanh")
        bias_scaled = sem("bias_scaled")
        st1, mv1, ve1, rs1, xn1 = (sem(n) for n in ("st1", "mv1", "ve1", "rs1", "xn1"))
        st2, mv2, ve2, rs2, xn2s = (sem(n) for n in ("st2", "mv2", "ve2", "rs2", "xn2s"))
        xb_done = sem("xb_done")
        ctx_replicated = sem("ctx_replicated")
        v_padded = sem("v_padded")
        xT_done, qT_saved = sem("xT_done"), sem("qT_saved")
        kT_done, kT_saved, k_diag_done = sem("kT_done"), sem("kT_saved"), sem("k_diag_done")
        scored, maxed, exped, inverted, normed = (sem(n) for n in ("scored", "maxed", "exped", "inverted", "normed"))
        pT_done, pT_saved_even, pT_saved_odd = sem("pT_done"), sem("pT_saved_even"), sem("pT_saved_odd")
        pv_done, oT_saved = sem("pv_done"), sem("oT_saved")
        wc_done, x1_done = sem("wc_done"), sem("x1_done")
        x2T_done, x2T_saved = sem("x2T_done"), sem("x2T_saved")
        logits_done, logits_saved, logits_turned = (sem(n) for n in ("logits_done", "logits_saved", "logits_turned"))
        xn2_stored = sem("xn2_stored")
        table_zeroed, table_scattered, table_read = sem("table_zeroed"), sem("table_scattered"), sem("table_read")
        picked_done, ranked, ranks_read = sem("picked_done"), sem("ranked"), sem("ranks_read")
        route = sem("route")
        gap_done, gap_exped, weights_done = sem("gap_done"), sem("gap_exped"), sem("weights_done")
        ids_done, rows_done, experts_done = sem("ids_done"), sem("rows_done"), sem("experts_done")
        sg_done, su_done, silu_s_done, hidT_s_done, down_s_done, x1s_done = (
            sem(n) for n in ("sg_done", "su_done", "silu_s_done", "hidT_s_done", "down_s_done", "x1s_done"))
        fetched = [sem(f"fetched{n}") for n in range(RING)]
        tokens_copied = sem("tokens_copied")
        xgT_done, xgT_saved, up_done, silu_done, hid_done = (
            sem(n) for n in ("xgT_done", "xgT_saved", "up_done", "silu_done", "hid_done"))
        hidT_done, hidT_saved, y_done, y_saved = (sem(n) for n in ("hidT_done", "hidT_saved", "y_done", "y_saved"))
        y_stored = [sem(f"y_stored{n}") for n in range(2)]
        y_fetched = [sem(f"y_fetched{n}") for n in range(2)]
        added1, added2 = sem("added1"), sem("added2")
        out_stored = sem("out_stored")

        waited = {eng.engine: sem(f"waited_{n}")
                  for n, eng in (("sp", nc.sync), ("pool", nc.gpsimd), ("pe", nc.tensor), ("dve", nc.vector))}

        block = stack.enter_context(nc.Block())

        def apart(eng):
            eng.sem_inc(waited[eng.engine], 1)

        def batch_steps(eng, step):
            for i in range(LAG + 1):
                step(i, i % 2)
            with eng.Fori(0, (B - LAG - 3) // 2) as k:
                for u in range(2):
                    step(k * 2 + (LAG + 1 + u), u)
            for i in range(B - 2, B + LAG):
                step(i, i % 2)

        def has(i, back):
            return 0 <= i - back < B if isinstance(i, int) else True

        def tile_steps(eng, step, last=NT + 2):
            turns = NT // RING - 1
            for t in range(RING):
                step(t, t, 0)
            with eng.Fori(0, turns) as k:
                for n in range(RING):
                    step(k * RING + (RING + n), n, k + 1)
            for t in range(RING * (turns + 1), last):
                step(t, t % RING, t // RING)

        def tile_has(t, back):
            return 0 <= t - back < NT if isinstance(t, int) else True

        @block.sync
        def _(sp):
            def load_batch(b, u):
                need(sp, x_loaded, b * 16)
                apart(sp)
                sp.dma_start(xs[:, bass.ds(b, 1), :],
                             x_tiles[bass.ds(b, 1)].rearrange("a p d -> p a d")).then_inc(x_loaded, 16)
                need(sp, ctx_loaded, b * 16)
                apart(sp)
                need(sp, ctx_replicated, b - 1)
                need(sp, v_padded, b - 1)
                apart(sp)
                sp.dma_start(ctxs[:, u:u + 1, :],
                             ctx_tiles[bass.ds(b, 1)].rearrange("a p d -> p a d")).then_inc(ctx_loaded, 16)

            def store_xn2(b, u):
                need(sp, xn2s, b + 1)
                apart(sp)
                need(sp, xn2_stored, b * 16)
                apart(sp)
                sp.dma_start(xn_tiles[bass.ds(b, 1)].rearrange("a p d -> p a d"),
                             xn2[:, u:u + 1, :]).then_inc(xn2_stored, 16)

            def step(i, u):
                if has(i, -2):
                    load_batch(i + 2, u)
                if has(i, 2):
                    store_xn2(i - 2, u)

            load_batch(0, 0)
            with nc.allow_non_contiguous_dma(reason="the gates"):
                sp.dma_start(tanh_g[:, 0:1], g_xattn.rearrange("(a o) -> a o", a=1).to_broadcast([P, 1])).then_inc(loaded, 16)
                sp.dma_start(tanh_g[:, 1:2], g_ffn.rearrange("(a o) -> a o", a=1).to_broadcast([P, 1])).then_inc(loaded, 16)
                sp.dma_start(bias_out, bc.rearrange("(a o) -> a o", a=1).to_broadcast([P, D])).then_inc(loaded, 16)
                sp.dma_start(gates[:, :, 0:E], gate_t.rearrange("(c p) e -> p c e", p=P)).then_inc(loaded, 16)
                sp.dma_start(gates[:, :, E:E + 1], sgate_t.rearrange("(c p) e -> p c e", p=P)).then_inc(loaded, 16)
            sp.dma_start(wc, wc_t.rearrange("(j p) n -> p j n", p=P)).then_inc(wc_loaded, 16)
            load_batch(1, 1)
            batch_steps(sp, step)
            sp.dma_start(ws_gate[:, :, :], wsg_t.rearrange("(c p) n -> p c n", p=P)).then_inc(shared_loaded, 16)
            sp.dma_start(ws_up[:, :, :], wsu_t.rearrange("(c p) n -> p c n", p=P)).then_inc(shared_loaded, 16)
            sp.dma_start(ws_down[:, :, :], wsd_t.rearrange("(c p) n -> p c n", p=P)).then_inc(shared_loaded, 16)
            sp.wait_ge(experts_done, 1)
            sp.wait_ge(xn2_stored, 16 * B)
            sp.wait_ge(table_zeroed, 16)
            sp.dma_start(experts[:, 0:E * DC * 2 * I], w13_t).then_inc(w13_loaded, 16)
            sp.wait_ge(table_scattered, 16 * TOPK * B)
            with nc.allow_non_contiguous_dma(reason="token numbers"):
                sp.dma_start(slot_token[:, :], table_slots).then_inc(table_read, 16)
            sp.dma_start(experts[:, E * DC * 2 * I:], w2_t).then_inc(w2_loaded, 16)

            def store_y(t, n, r):
                need(sp, y_saved, t + 1)
                apart(sp)
                sp.dma_start(y_slots[bass.ds(t, 1)].rearrange("a p d -> p a d"),
                             y_sb[:, n % 2:n % 2 + 1, :]).then_inc(y_stored[n % 2], 16)

            tile_steps(sp, store_y, NT)
            for b in range(B):
                sp.wait_ge(added2, b + 1)
                sp.dma_start(out_tiles[b], xs[:, b, :]).then_inc(out_stored, 16)
            sp.wait_ge(out_stored, 16 * B)

        @block.gpsimd
        def _(pool):
            pool.memset(minus_half[:, :], -0.5)
            pool.memset(ident[:, :], 0.0)
            pool.memset(ones_bf[:, :], 1.0)
            pool.memset(k_diag, 0.0)
            pool.memset(v_pad, 0.0)
            pool.memset(zeros_i, 0)
            pool.memset(tri_e, 1.0).then_inc(consts, 1)
            pool.wait_ge(consts, 1)
            pool.affine_select(out=ident[:, :], in_=ident[:, :], compare_op=ALU.not_equal, fill=1.0, base=0,
                               pattern=[[-1, P]], channel_multiplier=1).then_inc(consts_p, 1)
            pool.affine_select(out=strict_upper[:, :], in_=ones_bf[:, :], compare_op=ALU.is_gt, fill=0.0, base=0,
                               pattern=[[1, P]], channel_multiplier=-1).then_inc(consts_p, 1)
            tri = tri_e.rearrange("p (a b) -> p a b", a=E)
            pool.affine_select(out=tri, in_=tri, compare_op=ALU.is_gt, fill=0.0, base=0,
                               pattern=[[1, E], [-1, E]], channel_multiplier=0).then_inc(consts_p, 1)
            pool.iota(iota_e, [[1, E]], base=0, channel_multiplier=0, allow_small_or_imprecise_dtypes=True).then_inc(consts_p, 1)
            pool.iota(iota_t, [[1, NT]], base=0, channel_multiplier=0, allow_small_or_imprecise_dtypes=True).then_inc(consts_p, 1)
            pool.iota(token_id[:, :], [[P, B]], base=0, channel_multiplier=1).then_inc(consts_p, 1)
            pool.dma_start(table_slots, zeros_i).then_inc(table_zeroed, 16)

            def inverse_root(out_, in_, started, done, b):
                need(pool, started, b + 1)
                pool.tensor_tensor(out_, in_, minus_half[:, :], ALU.pow).then_inc(done, 1)

            def norm(b, g):
                need(pool, inverted, b * NG + g + 1)
                p4 = probs[:, g * D:(g + 1) * D].rearrange("p (j t) -> p j t", j=HG)
                s4 = inv_sum[:, g * HG:(g + 1) * HG].unsqueeze(2).to_broadcast([P, HG, P])
                pool.tensor_tensor(p4, p4, s4, ALU.mult).then_inc(normed, 1)

            def replicate_ctx(b, u):
                need(pool, ctx_loaded, b * 16 + 16)
                need(pool, kT_done, b)
                apart(pool)
                c = ctxs[:, u, :].rearrange("p (g r d) -> p g r d", g=NG, r=1).to_broadcast([P, NG, HG, HD])
                pool.tensor_copy(ctx_rep.rearrange("p (g r d) -> p g r d", g=NG, r=HG), c).then_inc(ctx_replicated, 1)
                need(pool, pv_done, b - 1)
                apart(pool)
                pool.tensor_copy(v_pad[:, u, :, 0:HD],
                                 ctxs[:, u, :].rearrange("p (g d) -> p g d", g=NG)).then_inc(v_padded, 1)

            def k_blocks(b):
                need(pool, kT_saved, b + 1)
                need(pool, scored, b * NG)
                apart(pool)
                kd = k_diag.rearrange("p (g j t) -> p g j t", g=NG, j=HG)
                ks = kT_rep.rearrange("p (g t) -> p g t", g=NG)
                for j in range(HG):
                    rows = slice(j * HD, (j + 1) * HD)
                    last = pool.tensor_copy(kd[rows, :, j, :], ks[rows])
                last.then_inc(k_diag_done, 1)
                need(pool, k_diag_done, b + 1)

            def add_bias(b):
                need(pool, xn1, b + 1)
                pool.tensor_tensor(xs[:, bass.ds(b, 1), :], xs[:, bass.ds(b, 1), :],
                                   bias_out.unsqueeze(1), ALU.add).then_inc(xb_done, 1)

            inverse_root(rstd1[:, 0:1], var1, ve1, rs1, 0)
            replicate_ctx(0, 0)
            pool.wait_ge(bias_scaled, 1)

            def step(i, u):
                if has(i, 1):
                    for g in range(NG):
                        norm(i - 1, g)
                if has(i, 2):
                    inverse_root(rstd2[:, 0:1], var2, ve2, rs2, i - 2)
                if has(i, -1):
                    inverse_root(rstd1[:, 0:1], var1, ve1, rs1, i + 1)
                if has(i, 0):
                    if has(i, -1):
                        need(pool, rs1, i + 2)
                    else:
                        need(pool, rs2, i - 1)
                    k_blocks(i)
                    add_bias(i)
                if has(i, -1):
                    replicate_ctx(i + 1, 1 - u)

            batch_steps(pool, step)

            pool.wait_ge(table_zeroed, 16)
            pool.wait_ge(rows_done, 1)
            for k in range(TOPK):
                for b in range(B):
                    pool.indirect_dma_start(
                        table_dram, bass.IndirectOffsetOnAxis(ap=slot_row[:, k, b:b + 1].bitcast(U32), axis=0),
                        token_id[:, b:b + 1], None).then_inc(table_scattered, 16)

            pool.wait_ge(table_read, 16)
            pool.wait_ge(xn2_stored, 16 * B)

            def fetch(t, n, r):
                need(pool, xgT_done, t - RING + 1)
                pool.tensor_copy(tokens_now[:, n:n + 1], slot_token[:, bass.ds(t, 1)]).then_inc(tokens_copied, 1)
                need(pool, tokens_copied, t + 1)
                apart(pool)
                pool.indirect_dma_start(
                    gathered[:, n, :], None, xn_dram,
                    bass.IndirectOffsetOnAxis(ap=tokens_now[:, n:n + 1].bitcast(U32), axis=0)).then_inc(fetched[n], 16)

            tile_steps(pool, fetch, NT)
            for n in range(2):
                pool.wait_ge(y_stored[n], 16 * ((NT + 1 - n) // 2))
            for b in range(B):
                n = b % 2
                if b >= 2:
                    pool.wait_ge(added2, b - 1)
                for k in range(TOPK):
                    pool.indirect_dma_start(
                        y_back[:, n, k, :], None, y_dram,
                        bass.IndirectOffsetOnAxis(ap=slot_row[:, k, b:b + 1].bitcast(U32), axis=0)).then_inc(y_fetched[n], 16)

        @block.tensor
        def _(pe):
            def four_transposes(dst, src):
                for c in range(4):
                    last = pe.transpose(dst[:, c * P:(c + 1) * P], src[:, c * P:(c + 1) * P], ident[:, :])
                return last

            def x_transpose(i, u):
                need(pe, xn1, i + 1)
                need(pe, pT_saved_odd, i * 2 - 2)
                if isinstance(i, int) and i == 1:
                    need(pe, qT_saved, 1)
                four_transposes(turn[0], xn[:, u, :]).then_inc(xT_done, 1)

            def k_transpose(i):
                need(pe, ctx_replicated, i + 1)
                need(pe, logits_saved, i - LAG)
                if isinstance(i, int) and i <= LAG:
                    need(pe, kT_saved, min(i, 1))
                    need(pe, pT_saved_even, i * 2 - 2)
                four_transposes(turn[1], ctx_rep).then_inc(kT_done, 1)

            def project(b, u):
                need(pe, oT_saved, b + 1)
                need(pe, x1_done, b)
                for j in range(HG):
                    mm = pe.matmul(wc_bank[:, :], oT[:, u, j * P:(j + 1) * P], wc[:, j, :],
                                   start=(j == 0), stop=(j == HG - 1))
                mm.then_inc(wc_done, 1)

            def x2_transpose(b, i, u):
                need(pe, xn2s, b + 1)
                if has(i, 0):
                    need(pe, qT_saved, i + 1)
                else:
                    need(pe, pT_saved_odd, min(i * 2 - 2, 2 * B))
                    need(pe, x2T_saved, b)
                four_transposes(turn[0], xn2[:, u, :]).then_inc(x2T_done, 1)

            def p_transpose(b, g):
                need(pe, normed, b * NG + g + 1)
                four_transposes(turn[1 - g % 2], probs[:, g * D:(g + 1) * D]).then_inc(pT_done, 1)

            def pv(b, g, u):
                need(pe, pT_saved_odd if g % 2 else pT_saved_even, b * 2 + g // 2 + 1)
                if g == 0:
                    need(pe, v_padded, b + 1)
                    need(pe, oT_saved, b)
                pad = v_pad[:, u, :, :].rearrange("p g c -> p (g c)")
                mm = pe.matmul(out_bank[:, :], pad[:, g * P:(g + 1) * P], probsT[:, g, :],
                               start=(g == 0), stop=(g == NG - 1))
                if g == NG - 1:
                    mm.then_inc(pv_done, 1)

            def router(b, i):
                need(pe, x2T_saved, b + 1)
                if isinstance(i, int) and not has(i, 1):
                    need(pe, logits_saved, b)
                for c in range(DC):
                    mm = pe.matmul(turn[1][0:E + 1, 0:P], gates[:, c, :], xnT[:, c, bass.ds(b * P, P)],
                                   start=(c == 0), stop=(c == DC - 1))
                mm.then_inc(logits_done, 1)

            def scores(i, u):
                need(pe, qT_saved, i + 1)
                need(pe, k_diag_done, i + 1)
                for g in range(NG):
                    need(pe, exped, i * NG + g + 1 - NG)
                    pe.matmul(bank[g][:, :], qT[:, u, g * P:(g + 1) * P], k_diag[:, g * D:(g + 1) * D],
                              start=True, stop=True).then_inc(scored, 1)

            def step(i, u):
                v = 1 - u
                if has(i, 0):
                    x_transpose(i, u)
                    k_transpose(i)
                if has(i, 2):
                    project(i - 2, u)
                if has(i, 3):
                    x2_transpose(i - 3, i, v)
                if has(i, 1):
                    b = i - 1
                    if has(i, 0):
                        need(pe, kT_saved, i + 1)
                    else:
                        need(pe, logits_saved, i - LAG)
                    p_transpose(b, 0)
                    if has(i, 3):
                        need(pe, x2T_saved, i - 2)
                    else:
                        need(pe, qT_saved, i + 1)
                    p_transpose(b, 1)
                    pv(b, 0, v)
                    p_transpose(b, 2)
                    pv(b, 1, v)
                    p_transpose(b, 3)
                    pv(b, 2, v)
                if has(i, 3):
                    router(i - 3, i)
                if has(i, 1):
                    pv(i - 1, 3, v)
                if has(i, 0):
                    scores(i, u)

            pe.wait_ge(consts_p, 2)
            pe.wait_ge(loaded, 16 * 5)
            pe.wait_ge(wc_loaded, 16)
            batch_steps(pe, step)

            need(pe, logits_saved, B)
            for b in range(B):
                last = pe.transpose(bank[2][:, b * (E + 1):(b + 1) * (E + 1)],
                                    logitsT[0:E + 1, b * P:(b + 1) * P], ident[0:E + 1, 0:E + 1])
            last.then_inc(logits_turned, 1)

            pe.wait_ge(picked_done, 1)
            pe.matmul(bank[0][:, 0:B * E], strict_upper[:, :], picked_any, start=True, stop=False, skip_group_check=True)
            for b in range(B - 1):
                left = B - 1 - b
                one = picked_any[:, b * E:(b + 1) * E].unsqueeze(1).to_broadcast([P, left, E])
                pe.matmul(bank[0][:, (b + 1) * E:B * E].rearrange("p (b e) -> p b e", e=E), ones_bf[:, :], one,
                          start=False, stop=(b == B - 2), skip_group_check=True)
            pe.matmul(bank[1][:, 0:B * E], ones_bf[:, :], picked_any, start=True, stop=True).then_inc(ranked, 1)

            pe.wait_ge(shared_loaded, 16 * 3)
            pe.wait_ge(ranks_read, 1)

            def shared_up(m, ic):
                for w, at, done in ((ws_gate, 0, sg_done), (ws_up, 2, su_done)):
                    need(pe, hidT_s_done, m * IC + ic - 1)
                    for c in range(DC):
                        mm = pe.matmul(bank[at + ic % 2][:, :], w[:, c, ic * P:(ic + 1) * P],
                                       xnT[:, c, bass.ds(m * MACRO, MACRO)], start=(c == 0), stop=(c == DC - 1))
                    mm.then_inc(done, 1)

            def shared_down(m, ic):
                need(pe, hidT_s_done, m * IC + ic + 1)
                for tt in range(TM):
                    if ic == 0:
                        need(pe, x1s_done, m * TM + tt + 1 - TM)
                    mm = pe.matmul(bank[4 + tt][:, :], hidT_s[:, ic % 2, tt * P:(tt + 1) * P], ws_down[:, ic, :],
                                   start=(ic == 0), stop=(ic == IC - 1))
                mm.then_inc(down_s_done, 1)

            def macro(m):
                for ic in range(IC):
                    shared_up(m, ic)
                    if ic > 0:
                        shared_down(m, ic - 1)
                    elif not isinstance(m, int) or m > 0:
                        shared_down(m - 1, IC - 1)

            macro(0)
            with pe.Fori(1, NM) as m:
                macro(m)
            shared_down(NM - 1, IC - 1)

            pe.wait_ge(w13_loaded, 16)
            pe.wait_ge(w2_loaded, 16)
            pe.wait_ge(x1s_done, B)

            def expert_of_tile(t):
                return pe.value_load(tile_expert[0:1, bass.ds(t, 1)], min_val=0, max_val=E - 1)

            def tile_step(t, n, r):
                u = n % 2
                if tile_has(t, 0):
                    need(pe, fetched[n], r * 16 + 16)
                    need(pe, xgT_saved, t - 1)
                    four_transposes(bank[u], gathered[:, n, :]).then_inc(xgT_done, 1)
                if tile_has(t, 2):
                    need(pe, hidT_saved, t - 1)
                    need(pe, y_saved, t - 3)
                    apart(pe)
                    e = expert_of_tile(t - 2)
                    pe.matmul(bank[2 + u][:, :], hidT[:, u, :], w2[:, bass.ds(e, 1), :],
                              start=True, stop=True).then_inc(y_done, 1)
                if tile_has(t, 1):
                    need(pe, hid_done, t)
                    need(pe, hidT_saved, t - 2)
                    pe.transpose(bank[7 - u][:, 0:P], hid[:, 1 - u, :], ident[:, :]).then_inc(hidT_done, 1)
                if tile_has(t, 0):
                    need(pe, xgT_saved, t + 1)
                    need(pe, hid_done, t - 1)
                    apart(pe)
                    e = expert_of_tile(t)
                    for c in range(DC):
                        mm = pe.matmul(bank[4 + u][:, 0:2 * I], xgT[:, u, c * P:(c + 1) * P],
                                       w13[:, bass.ds(e * DC + c, 1), :], start=(c == 0), stop=(c == DC - 1))
                    mm.then_inc(up_done, 1)

            tile_steps(pe, tile_step)

        @block.scalar
        def _(act):
            act.wait_ge(loaded, 16 * 5)
            nc.scalar.activation(tanh_g[:, :], tanh_g[:, :], ACT.Tanh).then_inc(gates_tanh, 1)

            def exps(b, g):
                need(act, maxed, b * NG + g + 1)
                need(act, pT_done, b * NG + g + 1 - NG)
                for j in range(HG):
                    h = g * HG + j
                    last = nc.scalar.activation(probs[:, h * P:(h + 1) * P], bank[g][:, j * P:(j + 1) * P], ACT.Exp,
                                                bias=neg_max[:, h:h + 1], accum_out=row_sum[:, h:h + 1])
                last.then_inc(exped, 1)

            def save_kT(i):
                need(act, kT_done, i + 1)
                need(act, k_diag_done, i)
                nc.scalar.activation(kT_rep, turn[1][:, :], ACT.Copy).then_inc(kT_saved, 1)

            def save_x2T(b):
                need(act, x2T_done, b + 1)
                nc.scalar.activation(xnT[:, :, bass.ds(b * P, P)], turn[0][:, :].rearrange("p (c n) -> p c n", c=DC),
                                     ACT.Copy).then_inc(x2T_saved, 1)

            def save_pT(b, g):
                need(act, pT_done, b * NG + g + 1)
                need(act, pv_done, b)
                nc.scalar.activation(probsT[:, g, :], turn[0][:, :], ACT.Copy).then_inc(pT_saved_odd, 1)

            def step(i, u):
                if has(i, 1):
                    exps(i - 1, 0)
                if has(i, 0):
                    save_kT(i)
                if has(i, 1):
                    for g in range(1, NG):
                        exps(i - 1, g)
                if has(i, 3):
                    save_x2T(i - 3)
                if has(i, 1):
                    save_pT(i - 1, 1)
                    save_pT(i - 1, 3)

            batch_steps(act, step)
            act.wait_ge(gap_done, 1)
            nc.scalar.activation(gap, gap, ACT.Exp).then_inc(gap_exped, 1)

            def silu_shared(m, ic):
                need(act, sg_done, m * IC + ic + 1)
                need(act, hidT_s_done, m * IC + ic - 1)
                nc.scalar.activation(silu_s[:, ic % 2, :], bank[ic % 2][:, :], ACT.Silu).then_inc(silu_s_done, 1)

            for ic in range(IC):
                silu_shared(0, ic)
            with act.Fori(1, NM) as m:
                for ic in range(IC):
                    silu_shared(m, ic)

            def tile_step(t, n, r):
                u = n % 2
                if tile_has(t, 0):
                    need(act, xgT_done, t + 1)
                    need(act, up_done, t - 1)
                    nc.scalar.activation(xgT[:, u, :], bank[u][:, :], ACT.Copy).then_inc(xgT_saved, 1)
                    need(act, up_done, t + 1)
                    need(act, hid_done, t - 1)
                    nc.scalar.activation(silu_c[:, u, :], bank[4 + u][:, 0:I], ACT.Silu).then_inc(silu_done, 1)

            tile_steps(act, tile_step)

        @block.vector
        def _(dve):
            dve.wait_ge(gates_tanh, 1)
            nc.vector.tensor_scalar(bias_out, bias_out, tanh_g[:, 0:1], None, ALU.mult).then_inc(bias_scaled, 1)

            def mean_var(x_, stats, mean, var, scale, st, mv, ve, b):
                nc.vector.bn_stats(stats, x_).then_inc(st, 1)
                need(dve, st, b + 1)
                apart(dve)
                nc.vector.bn_aggr(mean, stats).then_inc(mv, 1)
                need(dve, mv, b + 1)
                nc.vector.tensor_scalar(var, mean[:, 1:2], EPS, scale, ALU.add, ALU.mult).then_inc(ve, 1)

            def x_at(b):
                return xs[:, bass.ds(b, 1), :].rearrange("p a d -> p (a d)")

            def stats_x(b):
                need(dve, x_loaded, b * 16 + 16)
                apart(dve)
                mean_var(x_at(b), stats1, mean1, var1, float(HD), st1, mv1, ve1, b)

            def norm_x(b, u):
                need(dve, rs1, b + 1)
                nc.vector.tensor_scalar(xn[:, u, :], x_at(b), mean1[:, 0:1], rstd1[:, 0:1],
                                        ALU.subtract, ALU.mult).then_inc(xn1, 1)

            def max_of(b, g):
                need(dve, scored, b * NG + g + 1)
                nc.vector.tensor_reduce(neg_max[:, g * HG:(g + 1) * HG],
                                        bank[g][:, :].rearrange("p (j t) -> p j t", j=HG), AX.X, ALU.max,
                                        negate=True).then_inc(maxed, 1)

            def invert(b, g):
                need(dve, exped, b * NG + g + 1)
                nc.vector.reciprocal(inv_sum[:, g * HG:(g + 1) * HG],
                                     row_sum[:, g * HG:(g + 1) * HG]).then_inc(inverted, 1)

            def add_attention(b):
                need(dve, wc_done, b + 1)
                need(dve, xb_done, b + 1)
                nc.vector.scalar_tensor_tensor(x_at(b), wc_bank[:, :], tanh_g[:, 0:1], x_at(b),
                                               ALU.mult, ALU.add).then_inc(x1_done, 1)

            def stats_x1(b):
                need(dve, x1_done, b + 1)
                apart(dve)
                mean_var(x_at(b), stats2, mean2, var2, 1.0, st2, mv2, ve2, b)

            def norm_x1(b, u):
                need(dve, rs2, b + 1)
                need(dve, x2T_done, b - 1)
                need(dve, xn2_stored, b * 16 - 16)
                nc.vector.tensor_scalar(xn2[:, u, :], x_at(b), mean2[:, 0:1], rstd2[:, 0:1],
                                        ALU.subtract, ALU.mult).then_inc(xn2s, 1)

            def save_pT(b, g):
                need(dve, pT_done, b * NG + g + 1)
                need(dve, pv_done, b)
                nc.vector.tensor_copy(probsT[:, g, :], turn[1][:, :]).then_inc(pT_saved_even, 1)

            def step(i, u):
                v = 1 - u
                if has(i, 1):
                    max_of(i - 1, 0)
                    max_of(i - 1, 1)
                if has(i, 0):
                    need(dve, xT_done, i + 1)
                    nc.vector.tensor_copy(qT[:, u, :], turn[0][:, :]).then_inc(qT_saved, 1)
                if has(i, 1):
                    max_of(i - 1, 2)
                    max_of(i - 1, 3)
                    invert(i - 1, 0)
                    invert(i - 1, 1)
                if has(i, 2):
                    add_attention(i - 2)
                    stats_x1(i - 2)
                if has(i, 1):
                    invert(i - 1, 2)
                    invert(i - 1, 3)
                if has(i, -1):
                    stats_x(i + 1)
                if has(i, 1):
                    save_pT(i - 1, 0)
                if has(i, 2):
                    norm_x1(i - 2, u)
                if has(i, 1):
                    save_pT(i - 1, 2)
                if has(i, 3):
                    need(dve, logits_done, i - 2)
                    nc.vector.tensor_copy(logitsT[0:E + 1, bass.ds((i - 3) * P, P)],
                                          turn[1][0:E + 1, 0:P]).then_inc(logits_saved, 1)
                if has(i, 1):
                    need(dve, pv_done, i)
                    nc.vector.tensor_copy(oT[:, v, :], out_bank[:, :]).then_inc(oT_saved, 1)
                if has(i, -1):
                    norm_x(i + 1, v)

            stats_x(0)
            norm_x(0, 0)
            batch_steps(dve, step)

            count = [0]

            def then(ins):
                count[0] += 1
                ins.then_inc(route, 1)
                dve.wait_ge(route, count[0])

            dve.wait_ge(logits_turned, 1)
            dve.wait_ge(consts_p, 6)
            then(nc.vector.tensor_copy(logits, bank[2][:, 0:B * (E + 1)].rearrange("p (b e) -> p b e", b=B)))
            for b in range(B):
                last = nc.vector.max(top8[:, b, :], logits[:, b, 0:E])
            then(last)
            for b in range(B):
                last = nc.vector.max_index(top8_at[:, b, :], top8[:, b, :], logits[:, b, 0:E])
            then(last)
            then(nc.vector.tensor_copy(expert_of, top8_at[:, :, 0:TOPK].rearrange("p b k -> p k b")))
            for k in range(TOPK):
                last = nc.vector.tensor_tensor(
                    picked[:, k, :].rearrange("p (b e) -> p b e", b=B),
                    expert_of[:, k, :].unsqueeze(2).to_broadcast([P, B, E]),
                    iota_e.unsqueeze(1).to_broadcast([P, B, E]), ALU.is_equal)
            then(last)
            nc.vector.tensor_tensor(picked_any, picked[:, 0, :], picked[:, 1, :], ALU.add).then_inc(picked_done, 1)
            nc.vector.tensor_tensor(gap[:, 0:B], top8[:, :, 1], top8[:, :, 0], ALU.subtract)
            nc.vector.tensor_scalar(gap[:, B:2 * B], logits[:, :, E], -1.0, None, ALU.mult).then_inc(gap_done, 1)

            dve.wait_ge(ranked, 1)
            then(nc.vector.tensor_reduce(count_e, bank[1][:, 0:B * E].rearrange("p (b e) -> p e b", b=B), AX.X, ALU.add))
            then(nc.vector.tensor_scalar(tiles_e, count_e, 1.0 / P, (P - 1.0) / P - FLOOR, ALU.mult, ALU.add))
            then(nc.vector.tensor_copy(tiles_int, tiles_e))
            then(nc.vector.tensor_copy(tiles_e, tiles_int))
            then(nc.vector.tensor_tensor(before.rearrange("p (a b) -> p a b", a=E), tri_e.rearrange("p (a b) -> p a b", a=E),
                                         tiles_e.unsqueeze(1).to_broadcast([P, E, E]), ALU.mult))
            then(nc.vector.tensor_reduce(start_e, before.rearrange("p (a b) -> p a b", a=E), AX.X, ALU.add))
            then(nc.vector.tensor_tensor(end_e, start_e, tiles_e, ALU.add))
            then(nc.vector.tensor_scalar(place, bank[0][:, 0:B * E], 1.0 / P, -FLOOR, ALU.mult, ALU.add))
            then(nc.vector.tensor_copy(full_int, place))
            nc.vector.tensor_scalar(place, bank[0][:, 0:B * E], float(NT), None, ALU.mult).then_inc(ranks_read, 1)
            then(nc.vector.tensor_copy(full_tiles, full_int))
            then(nc.vector.scalar_tensor_tensor(place, full_tiles, 1.0 - P * NT, place, ALU.mult, ALU.add))
            then(nc.vector.tensor_tensor(place.rearrange("p (b e) -> p b e", b=B), place.rearrange("p (b e) -> p b e", b=B),
                                         start_e.unsqueeze(1).to_broadcast([P, B, E]), ALU.add))
            then(nc.vector.tensor_tensor(place_k, picked, place.unsqueeze(1).to_broadcast([P, TOPK, B * E]), ALU.mult))
            then(nc.vector.tensor_reduce(row_f, place_k.rearrange("p k (b e) -> p k b e", b=B), AX.X, ALU.add))
            nc.vector.tensor_copy(slot_row[:, :, :], row_f).then_inc(rows_done, 1)
            then(nc.vector.tensor_tensor(passed.rearrange("p (t e) -> p t e", e=E),
                                         end_e.unsqueeze(1).to_broadcast([P, NT, E]),
                                         iota_t.unsqueeze(2).to_broadcast([P, NT, E]), ALU.is_le))
            then(nc.vector.tensor_reduce(expert_f, passed.rearrange("p (t e) -> p t e", e=E), AX.X, ALU.add))
            then(nc.vector.tensor_scalar(expert_f, expert_f, E - 1.0, None, ALU.min))
            nc.vector.tensor_copy(tile_expert[:, :], expert_f)
            dve.wait_ge(gap_exped, 1)
            then(nc.vector.tensor_scalar(place[:, 0:2 * B], gap, 1.0, None, ALU.add))
            then(nc.vector.reciprocal(full_tiles[:, 0:2 * B], place[:, 0:2 * B]))
            then(nc.vector.tensor_scalar(weight[:, 0, :], full_tiles[:, 0:B], tanh_g[:, 1:2], None, ALU.mult))
            nc.vector.tensor_scalar(weight[:, 2, :], full_tiles[:, B:2 * B], tanh_g[:, 1:2], None, ALU.mult)
            then(nc.vector.tensor_tensor(weight[:, 1, :], weight[:, 0, :], gap[:, 0:B], ALU.mult))
            nc.vector.memset(expert_f[:, 0:1], 0.0).then_inc(experts_done, 1)

            def hidden_shared(m, ic):
                need(dve, silu_s_done, m * IC + ic + 1)
                need(dve, su_done, m * IC + ic + 1)
                need(dve, down_s_done, m * IC + ic - 1)
                nc.vector.tensor_tensor(hidT_s[:, ic % 2, :], bank[2 + ic % 2][:, :], silu_s[:, ic % 2, :],
                                        ALU.mult).then_inc(hidT_s_done, 1)

            def add_shared(m):
                need(dve, down_s_done, m * IC + IC)
                for tt in range(TM):
                    at = m * TM + tt
                    nc.vector.scalar_tensor_tensor(
                        x_at(at), bank[4 + tt][:, :], weight[:, 2, bass.ds(at, 1)], x_at(at),
                        ALU.mult, ALU.add).then_inc(x1s_done, 1)

            def macro(m):
                for ic in range(IC):
                    hidden_shared(m, ic)
                    if ic == 0 and not (isinstance(m, int) and m == 0):
                        add_shared(m - 1)

            macro(0)
            with dve.Fori(1, NM) as m:
                macro(m)
            add_shared(NM - 1)

            def tile_step(t, n, r):
                u = n % 2
                if tile_has(t, 2):
                    need(dve, y_done, t - 1)
                    if isinstance(t, int):
                        need(dve, y_stored[u], 16 * ((t - 2) // 2))
                    else:
                        need(dve, y_stored[u], r * 32 + 16 * ((n - 2) // 2))
                    nc.vector.tensor_copy(y_sb[:, u, :], bank[2 + u][:, :]).then_inc(y_saved, 1)
                if tile_has(t, 1):
                    need(dve, hidT_done, t)
                    need(dve, y_done, t - 2)
                    nc.vector.tensor_copy(hidT[:, 1 - u, :], bank[7 - u][:, 0:P]).then_inc(hidT_saved, 1)
                if tile_has(t, 0):
                    need(dve, silu_done, t + 1)
                    need(dve, hidT_done, t - 1)
                    nc.vector.tensor_tensor(hid[:, u, :], bank[4 + u][:, I:2 * I], silu_c[:, u, :],
                                            ALU.mult).then_inc(hid_done, 1)

            tile_steps(dve, tile_step)

            for b in range(B):
                n = b % 2
                dve.wait_ge(y_fetched[n], 16 * TOPK * (b // 2 + 1))
                for k, added in enumerate((added1, added2)):
                    if k:
                        dve.wait_ge(added1, b + 1)
                    nc.vector.scalar_tensor_tensor(xs[:, b, :], y_back[:, n, k, :], weight[:, k, b:b + 1], xs[:, b, :],
                                                   ALU.mult, ALU.add).then_inc(added, 1)


def kernel(x, ctx_512, g_xattn, g_ffn, L0_xattn_Wc, L0_xattn_bc, L0_ffn_gate_w, L0_ffn_w1, L0_ffn_w2, L0_ffn_w3,
           L0_ffn_ws_gate, L0_ffn_ws_up, L0_ffn_ws_down, L0_ffn_shared_gate_w):
    import numpy as np
    import concourse.bacc as bacc
    from concourse.bass_utils import run_bass_kernel_spmd

    def parts(w):
        e, n, h = w.shape
        return np.asarray(w).reshape(e, n, h // P, P).transpose(3, 0, 2, 1)

    arrays = {
        "x": np.asarray(x).reshape(B * P, D),
        "ctx": np.asarray(ctx_512).reshape(B * P, NG * HD),
        "g_xattn": np.asarray(g_xattn),
        "g_ffn": np.asarray(g_ffn),
        "wc_t": np.asarray(L0_xattn_Wc).T.reshape(NG, HG, HD, D).transpose(1, 0, 2, 3).reshape(D, D),
        "bc": np.asarray(L0_xattn_bc),
        "gate_t": np.asarray(L0_ffn_gate_w).T,
        "sgate_t": np.asarray(L0_ffn_shared_gate_w).T,
        "w13_t": np.concatenate([parts(L0_ffn_w1), parts(L0_ffn_w3)], axis=3).reshape(P, -1),
        "w2_t": np.asarray(L0_ffn_w2).transpose(2, 0, 1).reshape(P, -1),
        "wsg_t": np.asarray(L0_ffn_ws_gate).T,
        "wsu_t": np.asarray(L0_ffn_ws_up).T,
        "wsd_t": np.asarray(L0_ffn_ws_down).T,
    }
    nc = bacc.Bacc("TRN2", target_bir_lowering=False, num_devices=1)
    ins = {}
    for name in arrays:
        arrays[name] = np.ascontiguousarray(arrays[name])
        ins[name] = nc.dram_tensor(name, arrays[name].shape, mybir.dt.from_np(arrays[name].dtype), kind="ExternalInput").ap()
    xn_dram = nc.dram_tensor("xn_dram", [B * P, D], F32, kind="Internal").ap()
    y_dram = nc.dram_tensor("y_dram", [NT * P, D], F32, kind="Internal").ap()
    table_dram = nc.dram_tensor("table_dram", [NT * P, 1], I32, kind="Internal").ap()
    out = nc.dram_tensor("out", [B * P, D], F32, kind="ExternalOutput").ap()
    flamingo_block(nc, *ins.values(), xn_dram, y_dram, table_dram, out)
    r = run_bass_kernel_spmd(nc, [arrays], core_ids=[0])
    return r.results[0]["out"].reshape(B, P, D)
```

```python
from contextlib import ExitStack

import concourse.bass as bass
from concourse import mybir

F32 = mybir.dt.float32
BF16 = mybir.dt.bfloat16
I32 = mybir.dt.int32
U32 = mybir.dt.uint32
ALU = mybir.AluOpType
ACT = mybir.ActivationFunctionType
AX = mybir.AxisListType

P = 128
B = 16
D = 512
DC = D // P
NG = 4
HG = 4
HD = 32
H = NG * HG
E = 16
I = 128
IS = 512
IC = IS // P
TOPK = 2
NT = B * P * TOPK // P + E - 1
EPS = 1e-5
MACRO = 512
NM = B * P // MACRO
TM = MACRO // P
LAG = 3
RING = 4
FLOOR = 0.5 - 0.5 / P


def need(eng, sem, value):
    if isinstance(value, int) and value <= 0:
        return
    eng.wait_ge(sem, value)


def flamingo_block(nc, x, ctx, g_xattn, g_ffn, wc_t, bc, gate_t, sgate_t, w13_t, w2_t, wsg_t, wsu_t, wsd_t,
                   xn_dram, y_dram, table_dram, out):
    x_tiles = x.rearrange("(b p) d -> b p d", p=P)
    ctx_tiles = ctx.rearrange("(b p) d -> b p d", p=P)
    xn_tiles = xn_dram.rearrange("(b p) d -> b p d", p=P)
    out_tiles = out.rearrange("(b p) d -> b p d", p=P)
    y_slots = y_dram.rearrange("(p t) d -> t p d", t=NT)
    table_slots = table_dram.rearrange("(p t) o -> p (t o)", t=NT)

    with ExitStack() as stack:
        def sb(name, shape, dt=F32):
            return stack.enter_context(nc.sbuf_tensor(name, shape, dt))

        def sem(name):
            return stack.enter_context(nc.semaphore(name))

        xs = sb("xs", [P, B, D])
        xnT = sb("xnT", [P, DC, B * P])
        experts = sb("experts", [P, E * (DC * 2 * I + D)])
        w13 = experts[:, 0:E * DC * 2 * I].rearrange("p (ec n) -> p ec n", n=2 * I)
        w2 = experts[:, E * DC * 2 * I:E * (DC * 2 * I + D)].rearrange("p (e n) -> p e n", n=D)
        ws_gate = sb("ws_gate", [P, DC, IS])
        ws_up = sb("ws_up", [P, DC, IS])
        ws_down = sb("ws_down", [P, IC, D])
        shared = sb("shared", [P, 4 * D])
        wc = shared[:, :].rearrange("p (j n) -> p j n", j=HG)
        gates = sb("gates", [P, DC, E + 1])
        ident = sb("ident", [P, P])
        strict_upper = sb("strict_upper", [P, P], BF16)
        ones_bf = sb("ones_bf", [P, P], BF16)
        tanh_g = sb("tanh_g", [P, 2])
        minus_half = sb("minus_half", [P, 1])
        weight = sb("weight", [P, 3, B])
        slot_row = sb("slot_row", [P, TOPK, B], I32)
        token_id = sb("token_id", [P, B], I32)
        slot_token = sb("slot_token", [P, NT], I32)
        tokens_now = sb("tokens_now", [P, RING], I32)
        tile_expert = sb("tile_expert", [P, NT], I32)
        gathered = sb("gathered", [P, RING, D])
        silu_c = sb("silu_c", [P, 2, I])
        hid = sb("hid", [P, 2, I])
        hidT = sb("hidT", [P, 2, P])

        used = [0]

        def own(n, dt=F32):
            a = experts[:, used[0]:used[0] + n]
            used[0] += n
            return a if dt == F32 else a.bitcast(dt)

        qT = own(2 * D).rearrange("p (u n) -> p u n", u=2)
        ctxs = own(2 * P).rearrange("p (u n) -> p u n", u=2)
        ctx_rep = own(D)
        k_diag = own(NG * HG * P)
        v_pad = own(2 * NG * (P + HD)).rearrange("p (u g c) -> p u g c", u=2, g=NG)
        probs = own(H * P)
        probsT = own(NG * D).rearrange("p (g n) -> p g n", g=NG)
        oT = own(2 * D).rearrange("p (u n) -> p u n", u=2)
        xn = own(2 * D).rearrange("p (u n) -> p u n", u=2)
        xn2 = own(2 * D).rearrange("p (u n) -> p u n", u=2)
        bias_out = own(D)
        neg_max = own(H)
        row_sum = own(H)
        inv_sum = own(H)
        stats1, stats2 = own(6), own(6)
        mean1, mean2 = own(2), own(2)
        var1, var2 = own(1), own(1)
        rstd1, rstd2 = own(2), own(2)
        logitsT = own(B * P)
        logits = own(B * (E + 1)).rearrange("p (b e) -> p b e", b=B)
        top8 = own(B * 8).rearrange("p (b n) -> p b n", b=B)
        top8_at = own(B * 8, U32).rearrange("p (b n) -> p b n", b=B)
        expert_of = own(TOPK * B).rearrange("p (k b) -> p k b", k=TOPK)
        iota_e = own(E)
        iota_t = own(NT)
        tri_e = own(E * E)
        picked = own(TOPK * B * E).rearrange("p (k n) -> p k n", k=TOPK)
        picked_any = own(B * E // 2, BF16)
        count_e, tiles_e, start_e, end_e = own(E), own(E), own(E), own(E)
        tiles_int = own(E, I32)
        before = own(E * E)
        full_tiles = own(B * E)
        full_int = own(B * E, I32)
        place = own(B * E)
        place_k = own(TOPK * B * E).rearrange("p (k n) -> p k n", k=TOPK)
        row_f = own(TOPK * B).rearrange("p (k b) -> p k b", k=TOPK)
        passed = own(NT * E)
        expert_f = own(NT)
        zeros_i = own(NT, I32)
        gap = own(2 * B)
        assert used[0] <= E * (DC * 2 * I + D)
        silu_s = shared[:, 0:2 * MACRO].rearrange("p (u n) -> p u n", u=2)
        hidT_s = shared[:, 2 * MACRO:4 * MACRO].rearrange("p (u n) -> p u n", u=2)
        xgT = shared[:, 0:2 * D].rearrange("p (u n) -> p u n", u=2)
        y_sb = shared[:, 2 * D:4 * D].rearrange("p (u n) -> p u n", u=2)
        y_back = experts[:, 0:B // 2 * TOPK * D].rearrange("p (n k d) -> p n k d", k=TOPK, d=D)

        bank = [stack.enter_context(nc.psum_tensor(f"bank{i}", [P, 512], F32)) for i in range(8)]
        turn = [bank[4], bank[5]]
        out_bank, wc_bank = bank[6], bank[7]

        loaded = sem("loaded")
        wc_loaded = sem("wc_loaded")
        shared_loaded = sem("shared_loaded")
        x_loaded = sem("x_loaded")
        ctx_loaded = sem("ctx_loaded")
        w13_loaded = sem("w13_loaded")
        w2_loaded = sem("w2_loaded")
        consts = sem("consts")
        consts_p = sem("consts_p")
        ident_zeroed = sem("ident_zeroed")
        gates_tanh = sem("gates_tanh")
        bias_scaled = sem("bias_scaled")
        st1, mv1, ve1, rs1, xn1 = (sem(n) for n in ("st1", "mv1", "ve1", "rs1", "xn1"))
        st2, mv2, ve2, rs2, xn2s = (sem(n) for n in ("st2", "mv2", "ve2", "rs2", "xn2s"))
        xb_done = sem("xb_done")
        ctx_replicated = sem("ctx_replicated")
        v_padded = sem("v_padded")
        xT_done, qT_saved = sem("xT_done"), sem("qT_saved")
        kT_done, kT_saved = sem("kT_done"), sem("kT_saved")
        scored, maxed, exped, inverted, normed = (sem(n) for n in ("scored", "maxed", "exped", "inverted", "normed"))
        pT_done = sem("pT_done")
        pT_saved = [sem(f"pT_saved{g}") for g in range(NG)]
        pv_done, oT_saved = sem("pv_done"), sem("oT_saved")
        wc_done, x1_done = sem("wc_done"), sem("x1_done")
        x2T_done, x2T_saved = sem("x2T_done"), sem("x2T_saved")
        logits_done, logits_saved, logits_turned = (sem(n) for n in ("logits_done", "logits_saved", "logits_turned"))
        xn2_stored = sem("xn2_stored")
        table_zeroed, table_scattered, table_read = sem("table_zeroed"), sem("table_scattered"), sem("table_read")
        picked_done, ranked, ranks_read = sem("picked_done"), sem("ranked"), sem("ranks_read")
        route = sem("route")
        gap_done, gap_exped, weights_done = sem("gap_done"), sem("gap_exped"), sem("weights_done")
        ids_done, rows_done, experts_done = sem("ids_done"), sem("rows_done"), sem("experts_done")
        sg_done, su_done, silu_s_done, hidT_s_done, down_s_done, x1s_done = (
            sem(n) for n in ("sg_done", "su_done", "silu_s_done", "hidT_s_done", "down_s_done", "x1s_done"))
        fetched = [sem(f"fetched{n}") for n in range(RING)]
        tokens_copied = sem("tokens_copied")
        xgT_done, xgT_saved, up_done, silu_done, hid_done = (
            sem(n) for n in ("xgT_done", "xgT_saved", "up_done", "silu_done", "hid_done"))
        hidT_done, hidT_saved, y_done, y_saved = (sem(n) for n in ("hidT_done", "hidT_saved", "y_done", "y_saved"))
        y_stored = [sem(f"y_stored{n}") for n in range(2)]
        y_fetched = [sem(f"y_fetched{n}") for n in range(B // 2)]
        added1, added2 = sem("added1"), sem("added2")
        out_stored = sem("out_stored")

        waited = {eng.engine: sem(f"waited_{n}")
                  for n, eng in (("sp", nc.sync), ("pool", nc.gpsimd), ("pe", nc.tensor), ("dve", nc.vector))}

        block = stack.enter_context(nc.Block())

        def apart(eng):
            eng.sem_inc(waited[eng.engine], 1)

        def batch_steps(eng, step):
            for i in range(LAG + 1):
                step(i, i % 2)
            with eng.Fori(0, (B - LAG - 3) // 2) as k:
                for u in range(2):
                    step(k * 2 + (LAG + 1 + u), u)
            for i in range(B - 2, B + LAG):
                step(i, i % 2)

        def has(i, back):
            return 0 <= i - back < B if isinstance(i, int) else True

        def tile_steps(eng, step, last=NT + 2):
            turns = NT // RING - 1
            for t in range(RING):
                step(t, t, 0)
            with eng.Fori(0, turns) as k:
                for n in range(RING):
                    step(k * RING + (RING + n), n, k + 1)
            for t in range(RING * (turns + 1), last):
                step(t, t % RING, t // RING)

        def tile_has(t, back):
            return 0 <= t - back < NT if isinstance(t, int) else True

        @block.sync
        def _(sp):
            def load_batch(b, u):
                need(sp, x_loaded, b * 16)
                apart(sp)
                sp.dma_start(xs[:, bass.ds(b, 1), :],
                             x_tiles[bass.ds(b, 1)].rearrange("a p d -> p a d")).then_inc(x_loaded, 16)
                need(sp, ctx_loaded, b * 16)
                apart(sp)
                need(sp, ctx_replicated, b - 1)
                need(sp, v_padded, b - 1)
                apart(sp)
                sp.dma_start(ctxs[:, u:u + 1, :],
                             ctx_tiles[bass.ds(b, 1)].rearrange("a p d -> p a d")).then_inc(ctx_loaded, 16)

            def store_xn2(b, u):
                need(sp, xn2s, b + 1)
                apart(sp)
                need(sp, xn2_stored, b * 16)
                apart(sp)
                sp.dma_start(xn_tiles[bass.ds(b, 1)].rearrange("a p d -> p a d"),
                             xn2[:, u:u + 1, :]).then_inc(xn2_stored, 16)

            def step(i, u):
                if has(i, -2):
                    load_batch(i + 2, u)
                if has(i, 3):
                    store_xn2(i - 3, 1 - u)

            load_batch(0, 0)
            with nc.allow_non_contiguous_dma(reason="the gates"):
                sp.dma_start(tanh_g[:, 0:1], g_xattn.rearrange("(a o) -> a o", a=1).to_broadcast([P, 1])).then_inc(loaded, 16)
                sp.dma_start(tanh_g[:, 1:2], g_ffn.rearrange("(a o) -> a o", a=1).to_broadcast([P, 1])).then_inc(loaded, 16)
                sp.dma_start(bias_out, bc.rearrange("(a o) -> a o", a=1).to_broadcast([P, D])).then_inc(loaded, 16)
                sp.dma_start(gates[:, :, 0:E], gate_t.rearrange("(c p) e -> p c e", p=P)).then_inc(loaded, 16)
                sp.dma_start(gates[:, :, E:E + 1], sgate_t.rearrange("(c p) e -> p c e", p=P)).then_inc(loaded, 16)
            sp.dma_start(wc, wc_t.rearrange("(j p) n -> p j n", p=P)).then_inc(wc_loaded, 16)
            load_batch(1, 1)
            batch_steps(sp, step)
            sp.dma_start(ws_gate[:, :, :], wsg_t.rearrange("(c p) n -> p c n", p=P)).then_inc(shared_loaded, 16)
            sp.dma_start(ws_up[:, :, :], wsu_t.rearrange("(c p) n -> p c n", p=P)).then_inc(shared_loaded, 16)
            sp.dma_start(ws_down[:, :, :], wsd_t.rearrange("(c p) n -> p c n", p=P)).then_inc(shared_loaded, 16)
            sp.wait_ge(experts_done, 1)
            sp.wait_ge(xn2_stored, 16 * B)
            sp.wait_ge(table_zeroed, 16)
            sp.dma_start(experts[:, 0:E * DC * 2 * I], w13_t).then_inc(w13_loaded, 16)
            sp.wait_ge(table_scattered, 16 * TOPK * B)
            with nc.allow_non_contiguous_dma(reason="token numbers"):
                sp.dma_start(slot_token[:, :], table_slots).then_inc(table_read, 16)
            sp.dma_start(experts[:, E * DC * 2 * I:], w2_t).then_inc(w2_loaded, 16)

            def store_y(t, n, r):
                need(sp, y_saved, t + 1)
                apart(sp)
                sp.dma_start(y_slots[bass.ds(t, 1)].rearrange("a p d -> p a d"),
                             y_sb[:, n % 2:n % 2 + 1, :]).then_inc(y_stored[n % 2], 16)

            tile_steps(sp, store_y, NT)
            for b in range(B):
                sp.wait_ge(added2, b + 1)
                sp.wait_ge(x1s_done, b + 1)
                sp.dma_start(out_tiles[b], xs[:, b, :]).then_inc(out_stored, 16)
            sp.wait_ge(out_stored, 16 * B)

        @block.gpsimd
        def _(pool):
            pool.memset(minus_half[:, :], -0.5)
            pool.memset(ident[:, :], 0.0)
            pool.memset(ones_bf[:, :], 1.0)
            pool.memset(k_diag, 0.0)
            pool.memset(v_pad, 0.0)
            pool.memset(zeros_i, 0)
            pool.memset(tri_e, 1.0).then_inc(consts, 1)
            pool.wait_ge(consts, 1)
            pool.affine_select(out=ident[:, :], in_=ident[:, :], compare_op=ALU.not_equal, fill=1.0, base=0,
                               pattern=[[-1, P]], channel_multiplier=1).then_inc(consts_p, 1)
            pool.affine_select(out=strict_upper[:, :], in_=ones_bf[:, :], compare_op=ALU.is_gt, fill=0.0, base=0,
                               pattern=[[1, P]], channel_multiplier=-1).then_inc(consts_p, 1)
            tri = tri_e.rearrange("p (a b) -> p a b", a=E)
            pool.affine_select(out=tri, in_=tri, compare_op=ALU.is_gt, fill=0.0, base=0,
                               pattern=[[1, E], [-1, E]], channel_multiplier=0).then_inc(consts_p, 1)
            pool.iota(iota_e, [[1, E]], base=0, channel_multiplier=0, allow_small_or_imprecise_dtypes=True).then_inc(consts_p, 1)
            pool.iota(iota_t, [[1, NT]], base=0, channel_multiplier=0, allow_small_or_imprecise_dtypes=True).then_inc(consts_p, 1)
            pool.iota(token_id[:, :], [[P, B]], base=0, channel_multiplier=1).then_inc(consts_p, 1)
            pool.dma_start(table_slots, zeros_i).then_inc(table_zeroed, 16)

            def inverse_root(out_, in_, started, done, b):
                need(pool, started, b + 1)
                pool.tensor_tensor(out_, in_, minus_half[:, :], ALU.pow).then_inc(done, 1)

            def norm(b, g):
                need(pool, inverted, b * NG + g + 1)
                p4 = probs[:, g * D:(g + 1) * D].rearrange("p (j t) -> p j t", j=HG)
                s4 = inv_sum[:, g * HG:(g + 1) * HG].unsqueeze(2).to_broadcast([P, HG, P])
                pool.tensor_tensor(p4, p4, s4, ALU.mult).then_inc(normed, 1)

            def pad_values(b, u):
                need(pool, ctx_loaded, b * 16 + 16)
                need(pool, pv_done, b - 1)
                apart(pool)
                pool.tensor_copy(v_pad[:, u, :, 0:HD],
                                 ctxs[:, u, :].rearrange("p (g d) -> p g d", g=NG)).then_inc(v_padded, 1)

            def add_bias(b):
                need(pool, xn1, b + 1)
                pool.tensor_tensor(xs[:, bass.ds(b, 1), :], xs[:, bass.ds(b, 1), :],
                                   bias_out.unsqueeze(1), ALU.add).then_inc(xb_done, 1)

            inverse_root(rstd1[:, 0:1], var1, ve1, rs1, 0)
            pad_values(0, 0)
            pool.wait_ge(bias_scaled, 1)

            def step(i, u):
                if has(i, 1):
                    for g in range(NG):
                        norm(i - 1, g)
                if has(i, 2):
                    inverse_root(rstd2[:, 0:1], var2, ve2, rs2, i - 2)
                if has(i, -1):
                    inverse_root(rstd1[:, 0:1], var1, ve1, rs1, i + 1)
                if has(i, 0):
                    add_bias(i)
                if has(i, -1):
                    pad_values(i + 1, 1 - u)

            batch_steps(pool, step)

            pool.wait_ge(table_zeroed, 16)
            pool.wait_ge(rows_done, 1)
            for k in range(TOPK):
                for b in range(B):
                    pool.indirect_dma_start(
                        table_dram, bass.IndirectOffsetOnAxis(ap=slot_row[:, k, b:b + 1].bitcast(U32), axis=0),
                        token_id[:, b:b + 1], None).then_inc(table_scattered, 16)

            pool.wait_ge(table_read, 16)
            pool.wait_ge(xn2_stored, 16 * B)

            def fetch(t, n, r):
                need(pool, xgT_done, t - RING + 1)
                pool.tensor_copy(tokens_now[:, n:n + 1], slot_token[:, bass.ds(t, 1)]).then_inc(tokens_copied, 1)
                need(pool, tokens_copied, t + 1)
                apart(pool)
                pool.indirect_dma_start(
                    gathered[:, n, :], None, xn_dram,
                    bass.IndirectOffsetOnAxis(ap=tokens_now[:, n:n + 1].bitcast(U32), axis=0)).then_inc(fetched[n], 16)

            tile_steps(pool, fetch, NT)
            for n in range(2):
                pool.wait_ge(y_stored[n], 16 * ((NT + 1 - n) // 2))
            for b in range(B):
                n = b % (B // 2)
                if b >= B // 2:
                    pool.wait_ge(added2, n + 1)
                for k in range(TOPK):
                    pool.indirect_dma_start(
                        y_back[:, n, k, :], None, y_dram,
                        bass.IndirectOffsetOnAxis(ap=slot_row[:, k, b:b + 1].bitcast(U32), axis=0)).then_inc(y_fetched[n], 16)

        @block.tensor
        def _(pe):
            def four_transposes(dst, src):
                for c in range(4):
                    last = pe.transpose(dst[:, c * P:(c + 1) * P], src[:, c * P:(c + 1) * P], ident[:, :])
                return last

            def x_transpose(i, u):
                need(pe, xn1, i + 1)
                need(pe, pT_saved[3], i - 1)
                if isinstance(i, int) and i == 1:
                    need(pe, qT_saved, 1)
                four_transposes(turn[0], xn[:, u, :]).then_inc(xT_done, 1)

            def k_transpose(i):
                need(pe, ctx_replicated, i + 1)
                need(pe, pT_saved[2], i - 1)
                if isinstance(i, int) and i == 1:
                    need(pe, kT_saved, 1)
                four_transposes(turn[1], ctx_rep).then_inc(kT_done, 1)

            def project(b, u, half):
                need(pe, oT_saved, b + 1)
                need(pe, x1_done, b)
                for j in range(half * 2, half * 2 + 2):
                    mm = pe.matmul(wc_bank[:, :], oT[:, u, j * P:(j + 1) * P], wc[:, j, :],
                                   start=(j == 0), stop=(j == HG - 1))
                if half == 1:
                    mm.then_inc(wc_done, 1)

            def x2_transpose(b, i, u):
                need(pe, xn2s, b + 1)
                if has(i, 0):
                    need(pe, qT_saved, i + 1)
                else:
                    need(pe, pT_saved[3], min(i - 1, B))
                    need(pe, x2T_saved, b)
                four_transposes(turn[0], xn2[:, u, :]).then_inc(x2T_done, 1)

            def p_transpose(b, g):
                need(pe, normed, b * NG + g + 1)
                four_transposes(turn[1 - g % 2], probs[:, g * D:(g + 1) * D]).then_inc(pT_done, 1)

            def pv(b, g, u):
                need(pe, pT_saved[g], b + 1)
                if g == 0:
                    need(pe, v_padded, b + 1)
                    need(pe, oT_saved, b)
                pad = v_pad[:, u, :, :].rearrange("p g c -> p (g c)")
                mm = pe.matmul(out_bank[:, :], pad[:, g * P:(g + 1) * P], probsT[:, g, :],
                               start=(g == 0), stop=(g == NG - 1))
                if g == NG - 1:
                    mm.then_inc(pv_done, 1)

            def router(b, i):
                need(pe, x2T_saved, b + 1)
                need(pe, exped, NG * (min(i, B) if isinstance(i, int) else i))
                need(pe, logits_saved, b)
                for c in range(DC):
                    mm = pe.matmul(bank[3][0:E + 1, 0:P], gates[:, c, :], xnT[:, c, bass.ds(b * P, P)],
                                   start=(c == 0), stop=(c == DC - 1))
                mm.then_inc(logits_done, 1)

            def scores(i, u):
                need(pe, qT_saved, i + 1)
                need(pe, kT_saved, i + 1)
                for g in range(NG):
                    need(pe, exped, i * NG + g + 1 - NG)
                    if g == NG - 1:
                        need(pe, logits_saved, i - LAG + 1)
                    pe.matmul(bank[g][:, :], qT[:, u, g * P:(g + 1) * P], k_diag[:, g * D:(g + 1) * D],
                              start=True, stop=True).then_inc(scored, 1)

            def step(i, u):
                v = 1 - u
                if has(i, 0):
                    x_transpose(i, u)
                    k_transpose(i)
                if has(i, 2):
                    project(i - 2, u, 0)
                if has(i, 3):
                    x2_transpose(i - 3, i, v)
                if has(i, 2):
                    project(i - 2, u, 1)
                if has(i, 1):
                    b = i - 1
                    if has(i, 0):
                        need(pe, kT_saved, i + 1)
                    else:
                        need(pe, pT_saved[2], i - 1)
                    p_transpose(b, 0)
                    if has(i, 3):
                        need(pe, x2T_saved, i - 2)
                    else:
                        need(pe, qT_saved, i + 1)
                    p_transpose(b, 1)
                if has(i, 3):
                    router(i - 3, i)
                if has(i, 1):
                    pv(i - 1, 0, v)
                if has(i, 0):
                    scores(i, u)
                if has(i, 1):
                    p_transpose(b, 2)
                    pv(b, 1, v)
                    p_transpose(b, 3)
                    pv(b, 2, v)
                    pv(b, 3, v)

            pe.wait_ge(consts_p, 2)
            pe.wait_ge(loaded, 16 * 5)
            pe.wait_ge(wc_loaded, 16)
            batch_steps(pe, step)

            need(pe, logits_saved, B)
            for b in range(B):
                last = pe.transpose(bank[2][:, b * (E + 1):(b + 1) * (E + 1)],
                                    logitsT[0:E + 1, b * P:(b + 1) * P], ident[0:E + 1, 0:E + 1])
            last.then_inc(logits_turned, 1)

            pe.wait_ge(picked_done, 1)
            pe.matmul(bank[0][:, 0:B * E], strict_upper[:, :], picked_any, start=True, stop=False, skip_group_check=True)
            for b in range(B - 1):
                left = B - 1 - b
                one = picked_any[:, b * E:(b + 1) * E].unsqueeze(1).to_broadcast([P, left, E])
                pe.matmul(bank[0][:, (b + 1) * E:B * E].rearrange("p (b e) -> p b e", e=E), ones_bf[:, :], one,
                          start=False, stop=(b == B - 2), skip_group_check=True)
            pe.matmul(bank[1][:, 0:B * E], ones_bf[:, :], picked_any, start=True, stop=True).then_inc(ranked, 1)

            pe.wait_ge(shared_loaded, 16 * 3)
            pe.wait_ge(ranks_read, 1)

            def shared_up(m, ic):
                for w, at, done in ((ws_gate, 0, sg_done), (ws_up, 2, su_done)):
                    need(pe, hidT_s_done, m * IC + ic - 1)
                    for c in range(DC):
                        mm = pe.matmul(bank[at + ic % 2][:, :], w[:, c, ic * P:(ic + 1) * P],
                                       xnT[:, c, bass.ds(m * MACRO, MACRO)], start=(c == 0), stop=(c == DC - 1))
                    mm.then_inc(done, 1)

            def shared_down(m, ic):
                need(pe, hidT_s_done, m * IC + ic + 1)
                for tt in range(TM):
                    if ic == 0:
                        need(pe, x1s_done, m * TM + tt + 1 - TM)
                    mm = pe.matmul(bank[4 + tt][:, :], hidT_s[:, ic % 2, tt * P:(tt + 1) * P], ws_down[:, ic, :],
                                   start=(ic == 0), stop=(ic == IC - 1))
                mm.then_inc(down_s_done, 1)

            def shared_macro(m):
                for ic in range(IC):
                    shared_up(m, ic)
                    if ic > 0:
                        shared_down(m, ic - 1)
                shared_down(m, IC - 1)

            for m in range(NM // 2):
                shared_macro(m)

            pe.wait_ge(w13_loaded, 16)
            pe.wait_ge(w2_loaded, 16)
            pe.wait_ge(x1s_done, B // 2)

            def expert_of_tile(t):
                return pe.value_load(tile_expert[0:1, bass.ds(t, 1)], min_val=0, max_val=E - 1)

            def tile_step(t, n, r):
                u = n % 2
                if tile_has(t, 0):
                    need(pe, fetched[n], r * 16 + 16)
                    need(pe, xgT_saved, t - 1)
                    four_transposes(bank[u], gathered[:, n, :]).then_inc(xgT_done, 1)
                if tile_has(t, 2):
                    need(pe, hidT_saved, t - 1)
                    need(pe, y_saved, t - 3)
                    apart(pe)
                    e = expert_of_tile(t - 2)
                    pe.matmul(bank[2 + u][:, :], hidT[:, u, :], w2[:, bass.ds(e, 1), :],
                              start=True, stop=True).then_inc(y_done, 1)
                if tile_has(t, 1):
                    need(pe, hid_done, t)
                    need(pe, hidT_saved, t - 2)
                    pe.transpose(bank[7 - u][:, 0:P], hid[:, 1 - u, :], ident[:, :]).then_inc(hidT_done, 1)
                if tile_has(t, 0):
                    need(pe, xgT_saved, t + 1)
                    need(pe, hid_done, t - 1)
                    apart(pe)
                    e = expert_of_tile(t)
                    for c in range(DC):
                        mm = pe.matmul(bank[4 + u][:, 0:2 * I], xgT[:, u, c * P:(c + 1) * P],
                                       w13[:, bass.ds(e * DC + c, 1), :], start=(c == 0), stop=(c == DC - 1))
                    mm.then_inc(up_done, 1)

            tile_steps(pe, tile_step)
            pe.wait_ge(y_saved, NT)
            with pe.Fori(NM // 2, NM) as m:
                shared_macro(m)

        @block.scalar
        def _(act):
            act.wait_ge(loaded, 16 * 5)
            nc.scalar.activation(tanh_g[:, :], tanh_g[:, :], ACT.Tanh).then_inc(gates_tanh, 1)

            def exps(b, g):
                need(act, maxed, b * NG + g + 1)
                need(act, pT_done, b * NG + g + 1 - NG)
                for j in range(HG):
                    h = g * HG + j
                    last = nc.scalar.activation(probs[:, h * P:(h + 1) * P], bank[g][:, j * P:(j + 1) * P], ACT.Exp,
                                                bias=neg_max[:, h:h + 1], accum_out=row_sum[:, h:h + 1])
                last.then_inc(exped, 1)

            def save_kT(i):
                need(act, kT_done, i + 1)
                need(act, scored, i * NG)
                kd = k_diag.rearrange("p (g j t) -> p g j t", g=NG, j=HG)
                ks = turn[1][:, :].rearrange("p (g t) -> p g t", g=NG)
                for j in range(HG):
                    rows = slice(j * HD, (j + 1) * HD)
                    last = nc.scalar.activation(kd[rows, :, j, :], ks[rows], ACT.Copy)
                last.then_inc(kT_saved, 1)

            def save_x2T(b):
                need(act, x2T_done, b + 1)
                nc.scalar.activation(xnT[:, :, bass.ds(b * P, P)], turn[0][:, :].rearrange("p (c n) -> p c n", c=DC),
                                     ACT.Copy).then_inc(x2T_saved, 1)

            def save_pT(b, g):
                need(act, pT_done, b * NG + g + 1)
                need(act, pv_done, b)
                nc.scalar.activation(probsT[:, g, :], turn[1 - g % 2][:, :], ACT.Copy).then_inc(pT_saved[g], 1)

            def step(i, u):
                if has(i, 1):
                    exps(i - 1, 0)
                if has(i, 2):
                    save_pT(i - 2, 2)
                    save_pT(i - 2, 3)
                if has(i, 1):
                    exps(i - 1, 1)
                    exps(i - 1, 2)
                if has(i, 0):
                    save_kT(i)
                if has(i, 3):
                    save_x2T(i - 3)
                if has(i, 1):
                    exps(i - 1, 3)
                    save_pT(i - 1, 1)

            batch_steps(act, step)
            act.wait_ge(gap_done, 1)
            nc.scalar.activation(gap, gap, ACT.Exp).then_inc(gap_exped, 1)

            def silu_shared(m, ic):
                need(act, sg_done, m * IC + ic + 1)
                need(act, hidT_s_done, m * IC + ic - 1)
                nc.scalar.activation(silu_s[:, ic % 2, :], bank[ic % 2][:, :], ACT.Silu).then_inc(silu_s_done, 1)

            for m in range(NM // 2):
                for ic in range(IC):
                    silu_shared(m, ic)

            def tile_step(t, n, r):
                u = n % 2
                if tile_has(t, 0):
                    need(act, xgT_done, t + 1)
                    need(act, up_done, t - 1)
                    nc.scalar.activation(xgT[:, u, :], bank[u][:, :], ACT.Copy).then_inc(xgT_saved, 1)
                    need(act, up_done, t + 1)
                    need(act, hid_done, t - 1)
                    nc.scalar.activation(silu_c[:, u, :], bank[4 + u][:, 0:I], ACT.Silu).then_inc(silu_done, 1)

            tile_steps(act, tile_step)
            with act.Fori(NM // 2, NM) as m:
                for ic in range(IC):
                    silu_shared(m, ic)

        @block.vector
        def _(dve):
            dve.wait_ge(gates_tanh, 1)
            nc.vector.tensor_scalar(bias_out, bias_out, tanh_g[:, 0:1], None, ALU.mult).then_inc(bias_scaled, 1)

            def mean_var(x_, stats, mean, var, scale, st, mv, ve, b):
                nc.vector.bn_stats(stats, x_).then_inc(st, 1)
                need(dve, st, b + 1)
                apart(dve)
                nc.vector.bn_aggr(mean, stats).then_inc(mv, 1)
                need(dve, mv, b + 1)
                nc.vector.tensor_scalar(var, mean[:, 1:2], EPS, scale, ALU.add, ALU.mult).then_inc(ve, 1)

            def x_at(b):
                return xs[:, bass.ds(b, 1), :].rearrange("p a d -> p (a d)")

            def stats_x(b):
                need(dve, x_loaded, b * 16 + 16)
                apart(dve)
                mean_var(x_at(b), stats1, mean1, var1, float(HD), st1, mv1, ve1, b)

            def replicate_keys(b, u):
                need(dve, ctx_loaded, b * 16 + 16)
                need(dve, kT_done, b)
                c = ctxs[:, u, :].rearrange("p (g r d) -> p g r d", g=NG, r=1).to_broadcast([P, NG, HG, HD])
                nc.vector.tensor_copy(ctx_rep.rearrange("p (g r d) -> p g r d", g=NG, r=HG), c).then_inc(ctx_replicated, 1)

            def norm_x(b, u):
                need(dve, rs1, b + 1)
                nc.vector.tensor_scalar(xn[:, u, :], x_at(b), mean1[:, 0:1], rstd1[:, 0:1],
                                        ALU.subtract, ALU.mult).then_inc(xn1, 1)

            def max_of(b, g):
                need(dve, scored, b * NG + g + 1)
                nc.vector.tensor_reduce(neg_max[:, g * HG:(g + 1) * HG],
                                        bank[g][:, :].rearrange("p (j t) -> p j t", j=HG), AX.X, ALU.max,
                                        negate=True).then_inc(maxed, 1)

            def invert(b, g):
                need(dve, exped, b * NG + g + 1)
                nc.vector.reciprocal(inv_sum[:, g * HG:(g + 1) * HG],
                                     row_sum[:, g * HG:(g + 1) * HG]).then_inc(inverted, 1)

            def add_attention(b):
                need(dve, wc_done, b + 1)
                need(dve, xb_done, b + 1)
                nc.vector.scalar_tensor_tensor(x_at(b), wc_bank[:, :], tanh_g[:, 0:1], x_at(b),
                                               ALU.mult, ALU.add).then_inc(x1_done, 1)

            def stats_x1(b):
                need(dve, x1_done, b + 1)
                apart(dve)
                mean_var(x_at(b), stats2, mean2, var2, 1.0, st2, mv2, ve2, b)

            def norm_x1(b, u):
                need(dve, rs2, b + 1)
                need(dve, x2T_done, b - 1)
                need(dve, xn2_stored, b * 16 - 16)
                nc.vector.tensor_scalar(xn2[:, u, :], x_at(b), mean2[:, 0:1], rstd2[:, 0:1],
                                        ALU.subtract, ALU.mult).then_inc(xn2s, 1)

            def save_pT(b, g):
                need(dve, pT_done, b * NG + g + 1)
                need(dve, pv_done, b)
                nc.vector.tensor_copy(probsT[:, g, :], turn[1][:, :]).then_inc(pT_saved[g], 1)

            def step(i, u):
                if has(i, 1):
                    max_of(i - 1, 0)
                    max_of(i - 1, 1)
                    invert(i - 1, 0)
                    max_of(i - 1, 2)
                if has(i, 0):
                    norm_x(i, u)
                if has(i, 1):
                    max_of(i - 1, 3)
                if has(i, 0):
                    replicate_keys(i, u)
                if has(i, 2):
                    need(dve, pv_done, i - 1)
                    nc.vector.tensor_copy(oT[:, u, :], out_bank[:, :]).then_inc(oT_saved, 1)
                if has(i, 0):
                    need(dve, xT_done, i + 1)
                    nc.vector.tensor_copy(qT[:, u, :], turn[0][:, :]).then_inc(qT_saved, 1)
                if has(i, 1):
                    invert(i - 1, 1)
                if has(i, 3):
                    norm_x1(i - 3, 1 - u)
                if has(i, 1):
                    invert(i - 1, 2)
                if has(i, -1):
                    stats_x(i + 1)
                if has(i, 1):
                    save_pT(i - 1, 0)
                    invert(i - 1, 3)
                if has(i, 3):
                    need(dve, logits_done, i - 2)
                    nc.vector.tensor_copy(logitsT[0:E + 1, bass.ds((i - 3) * P, P)],
                                          bank[3][0:E + 1, 0:P]).then_inc(logits_saved, 1)
                if has(i, 2):
                    add_attention(i - 2)
                    stats_x1(i - 2)

            stats_x(0)
            batch_steps(dve, step)

            count = [0]

            def then(ins):
                count[0] += 1
                ins.then_inc(route, 1)
                dve.wait_ge(route, count[0])

            dve.wait_ge(logits_turned, 1)
            dve.wait_ge(consts_p, 6)
            then(nc.vector.tensor_copy(logits, bank[2][:, 0:B * (E + 1)].rearrange("p (b e) -> p b e", b=B)))
            for b in range(B):
                last = nc.vector.max(top8[:, b, :], logits[:, b, 0:E])
            then(last)
            for b in range(B):
                last = nc.vector.max_index(top8_at[:, b, :], top8[:, b, :], logits[:, b, 0:E])
            then(last)
            then(nc.vector.tensor_copy(expert_of, top8_at[:, :, 0:TOPK].rearrange("p b k -> p k b")))
            for k in range(TOPK):
                last = nc.vector.tensor_tensor(
                    picked[:, k, :].rearrange("p (b e) -> p b e", b=B),
                    expert_of[:, k, :].unsqueeze(2).to_broadcast([P, B, E]),
                    iota_e.unsqueeze(1).to_broadcast([P, B, E]), ALU.is_equal)
            then(last)
            nc.vector.tensor_tensor(picked_any, picked[:, 0, :], picked[:, 1, :], ALU.add).then_inc(picked_done, 1)
            nc.vector.tensor_tensor(gap[:, 0:B], top8[:, :, 1], top8[:, :, 0], ALU.subtract)
            nc.vector.tensor_scalar(gap[:, B:2 * B], logits[:, :, E], -1.0, None, ALU.mult).then_inc(gap_done, 1)

            dve.wait_ge(ranked, 1)
            then(nc.vector.tensor_reduce(count_e, bank[1][:, 0:B * E].rearrange("p (b e) -> p e b", b=B), AX.X, ALU.add))
            then(nc.vector.tensor_scalar(tiles_e, count_e, 1.0 / P, (P - 1.0) / P - FLOOR, ALU.mult, ALU.add))
            then(nc.vector.tensor_copy(tiles_int, tiles_e))
            then(nc.vector.tensor_copy(tiles_e, tiles_int))
            then(nc.vector.tensor_tensor(before.rearrange("p (a b) -> p a b", a=E), tri_e.rearrange("p (a b) -> p a b", a=E),
                                         tiles_e.unsqueeze(1).to_broadcast([P, E, E]), ALU.mult))
            then(nc.vector.tensor_reduce(start_e, before.rearrange("p (a b) -> p a b", a=E), AX.X, ALU.add))
            then(nc.vector.tensor_tensor(end_e, start_e, tiles_e, ALU.add))
            then(nc.vector.tensor_scalar(place, bank[0][:, 0:B * E], 1.0 / P, -FLOOR, ALU.mult, ALU.add))
            then(nc.vector.tensor_copy(full_int, place))
            nc.vector.tensor_scalar(place, bank[0][:, 0:B * E], float(NT), None, ALU.mult).then_inc(ranks_read, 1)
            then(nc.vector.tensor_copy(full_tiles, full_int))
            then(nc.vector.scalar_tensor_tensor(place, full_tiles, 1.0 - P * NT, place, ALU.mult, ALU.add))
            then(nc.vector.tensor_tensor(place.rearrange("p (b e) -> p b e", b=B), place.rearrange("p (b e) -> p b e", b=B),
                                         start_e.unsqueeze(1).to_broadcast([P, B, E]), ALU.add))
            then(nc.vector.tensor_tensor(place_k, picked, place.unsqueeze(1).to_broadcast([P, TOPK, B * E]), ALU.mult))
            then(nc.vector.tensor_reduce(row_f, place_k.rearrange("p k (b e) -> p k b e", b=B), AX.X, ALU.add))
            nc.vector.tensor_copy(slot_row[:, :, :], row_f).then_inc(rows_done, 1)
            then(nc.vector.tensor_tensor(passed.rearrange("p (t e) -> p t e", e=E),
                                         end_e.unsqueeze(1).to_broadcast([P, NT, E]),
                                         iota_t.unsqueeze(2).to_broadcast([P, NT, E]), ALU.is_le))
            then(nc.vector.tensor_reduce(expert_f, passed.rearrange("p (t e) -> p t e", e=E), AX.X, ALU.add))
            then(nc.vector.tensor_scalar(expert_f, expert_f, E - 1.0, None, ALU.min))
            nc.vector.tensor_copy(tile_expert[:, :], expert_f)
            dve.wait_ge(gap_exped, 1)
            then(nc.vector.tensor_scalar(place[:, 0:2 * B], gap, 1.0, None, ALU.add))
            then(nc.vector.reciprocal(full_tiles[:, 0:2 * B], place[:, 0:2 * B]))
            then(nc.vector.tensor_scalar(weight[:, 0, :], full_tiles[:, 0:B], tanh_g[:, 1:2], None, ALU.mult))
            nc.vector.tensor_scalar(weight[:, 2, :], full_tiles[:, B:2 * B], tanh_g[:, 1:2], None, ALU.mult)
            then(nc.vector.tensor_tensor(weight[:, 1, :], weight[:, 0, :], gap[:, 0:B], ALU.mult))
            nc.vector.memset(expert_f[:, 0:1], 0.0).then_inc(experts_done, 1)

            def hidden_shared(m, ic):
                need(dve, silu_s_done, m * IC + ic + 1)
                need(dve, su_done, m * IC + ic + 1)
                need(dve, down_s_done, m * IC + ic - 1)
                nc.vector.tensor_tensor(hidT_s[:, ic % 2, :], bank[2 + ic % 2][:, :], silu_s[:, ic % 2, :],
                                        ALU.mult).then_inc(hidT_s_done, 1)

            def add_shared(m):
                need(dve, down_s_done, m * IC + IC)
                for tt in range(TM):
                    at = m * TM + tt
                    nc.vector.scalar_tensor_tensor(
                        x_at(at), bank[4 + tt][:, :], weight[:, 2, bass.ds(at, 1)], x_at(at),
                        ALU.mult, ALU.add).then_inc(x1s_done, 1)

            for m in range(NM // 2):
                for ic in range(IC):
                    hidden_shared(m, ic)
                add_shared(m)

            def tile_step(t, n, r):
                u = n % 2
                if tile_has(t, 2):
                    need(dve, y_done, t - 1)
                    if isinstance(t, int):
                        need(dve, y_stored[u], 16 * ((t - 2) // 2))
                    else:
                        need(dve, y_stored[u], r * 32 + 16 * ((n - 2) // 2))
                    nc.vector.tensor_copy(y_sb[:, u, :], bank[2 + u][:, :]).then_inc(y_saved, 1)
                if tile_has(t, 1):
                    need(dve, hidT_done, t)
                    need(dve, y_done, t - 2)
                    nc.vector.tensor_copy(hidT[:, 1 - u, :], bank[7 - u][:, 0:P]).then_inc(hidT_saved, 1)
                if tile_has(t, 0):
                    need(dve, silu_done, t + 1)
                    need(dve, hidT_done, t - 1)
                    nc.vector.tensor_tensor(hid[:, u, :], bank[4 + u][:, I:2 * I], silu_c[:, u, :],
                                            ALU.mult).then_inc(hid_done, 1)

            tile_steps(dve, tile_step)

            for n in range(2):
                dve.wait_ge(y_stored[n], 16 * ((NT + 1 - n) // 2))

            def add_routed(m, n):
                b = m * (B // 2) + n
                need(dve, y_fetched[n], m * (16 * TOPK) + 16 * TOPK)
                need(dve, x1s_done, m * TM + B // 2)
                for k, added in enumerate((added1, added2)):
                    if k:
                        need(dve, added1, b + 1)
                    nc.vector.scalar_tensor_tensor(x_at(b), y_back[:, n, k, :], weight[:, k, bass.ds(b, 1)], x_at(b),
                                                   ALU.mult, ALU.add).then_inc(added, 1)

            with dve.Fori(0, NM // 2) as m:
                for ic in range(IC):
                    hidden_shared(m + NM // 2, ic)
                    for j in range(2):
                        add_routed(m, ic * 2 + j)
                need(dve, added2, m * (B // 2) + B // 2)
                add_shared(m + NM // 2)


def kernel(x, ctx_512, g_xattn, g_ffn, L0_xattn_Wc, L0_xattn_bc, L0_ffn_gate_w, L0_ffn_w1, L0_ffn_w2, L0_ffn_w3,
           L0_ffn_ws_gate, L0_ffn_ws_up, L0_ffn_ws_down, L0_ffn_shared_gate_w):
    import numpy as np
    import concourse.bacc as bacc
    from concourse.bass_utils import run_bass_kernel_spmd

    def parts(w):
        e, n, h = w.shape
        return np.asarray(w).reshape(e, n, h // P, P).transpose(3, 0, 2, 1)

    arrays = {
        "x": np.asarray(x).reshape(B * P, D),
        "ctx": np.asarray(ctx_512).reshape(B * P, NG * HD),
        "g_xattn": np.asarray(g_xattn),
        "g_ffn": np.asarray(g_ffn),
        "wc_t": np.asarray(L0_xattn_Wc).T.reshape(NG, HG, HD, D).transpose(1, 0, 2, 3).reshape(D, D),
        "bc": np.asarray(L0_xattn_bc),
        "gate_t": np.asarray(L0_ffn_gate_w).T,
        "sgate_t": np.asarray(L0_ffn_shared_gate_w).T,
        "w13_t": np.concatenate([parts(L0_ffn_w1), parts(L0_ffn_w3)], axis=3).reshape(P, -1),
        "w2_t": np.asarray(L0_ffn_w2).transpose(2, 0, 1).reshape(P, -1),
        "wsg_t": np.asarray(L0_ffn_ws_gate).T,
        "wsu_t": np.asarray(L0_ffn_ws_up).T,
        "wsd_t": np.asarray(L0_ffn_ws_down).T,
    }
    nc = bacc.Bacc("TRN2", target_bir_lowering=False, num_devices=1)
    ins = {}
    for name in arrays:
        arrays[name] = np.ascontiguousarray(arrays[name])
        ins[name] = nc.dram_tensor(name, arrays[name].shape, mybir.dt.from_np(arrays[name].dtype), kind="ExternalInput").ap()
    xn_dram = nc.dram_tensor("xn_dram", [B * P, D], F32, kind="Internal").ap()
    y_dram = nc.dram_tensor("y_dram", [NT * P, D], F32, kind="Internal").ap()
    table_dram = nc.dram_tensor("table_dram", [NT * P, 1], I32, kind="Internal").ap()
    out = nc.dram_tensor("out", [B * P, D], F32, kind="ExternalOutput").ap()
    flamingo_block(nc, *ins.values(), xn_dram, y_dram, table_dram, out)
    r = run_bass_kernel_spmd(nc, [arrays], core_ids=[0])
    return r.results[0]["out"].reshape(B, P, D)
```

```python
from contextlib import ExitStack

import concourse.bass as bass
from concourse import mybir

F32 = mybir.dt.float32
F32R = mybir.dt.float32r
BF16 = mybir.dt.bfloat16
I32 = mybir.dt.int32
U32 = mybir.dt.uint32
ALU = mybir.AluOpType
ACT = mybir.ActivationFunctionType
AX = mybir.AxisListType

P = 128
B = 16
D = 512
DC = D // P
NG = 4
HG = 4
HD = 32
H = NG * HG
E = 16
I = 128
IS = 512
IC = IS // P
TOPK = 2
SPLIT_ORDER = (1, 0, 2, 3)
NT = B * P * TOPK // P + E - 1
EPS = 1e-5
MACRO = 512
NM = B * P // MACRO
TM = MACRO // P
LAG = 3
RING = 4
FLOOR = 0.5 - 0.5 / P


def need(eng, sem, value):
    if isinstance(value, int) and value <= 0:
        return
    eng.wait_ge(sem, value)


def flamingo_block(nc, x, ctx, keys_t, g_xattn, g_ffn, wc_t, bc, gate_t, sgate_t, w13_t, w2_t, wsg_t, wsu_t, wsd_t,
                   xn_dram, y_dram, out):
    x_tiles = x.rearrange("(b p) d -> b p d", p=P)
    ctx_tiles = ctx.rearrange("(b p) d -> b p d", p=P)
    key_tiles = keys_t.rearrange("(b d) n -> b d n", d=HD)
    xn_tiles = xn_dram.rearrange("(b p) d -> b p d", p=P)
    out_tiles = out.rearrange("(b p) d -> b p d", p=P)
    y_slots = y_dram.rearrange("(p t) d -> t p d", t=NT)

    with ExitStack() as stack:
        def sb(name, shape, dt=F32):
            return stack.enter_context(nc.sbuf_tensor(name, shape, dt))

        def sem(name):
            return stack.enter_context(nc.semaphore(name))

        xs = sb("xs", [P, B, D])
        xnT = sb("xnT", [P, DC, B * P])
        experts_at = nc.sbuf_base
        experts = sb("experts", [P, E * (DC * 2 * I + D)])
        w13 = experts[:, 0:E * DC * 2 * I].rearrange("p (ec n) -> p ec n", n=2 * I)
        w2 = experts[:, E * DC * 2 * I:E * (DC * 2 * I + D)].rearrange("p (e n) -> p e n", n=D)
        ws_gate = sb("ws_gate", [P, DC, IS])
        ws_up = sb("ws_up", [P, DC, IS])
        ws_down = sb("ws_down", [P, IC, D])
        shared_at = nc.sbuf_base
        shared = sb("shared", [P, 4 * D])
        gathered_at = nc.sbuf_base
        gathered = sb("gathered", [P, RING, D])
        gates = sb("gates", [P, DC, E + 1])
        ident = sb("ident", [P, P])
        strict_upper = sb("strict_upper", [P, P], BF16)
        ones_bf = sb("ones_bf", [P, P], BF16)
        tanh_g = sb("tanh_g", [P, 2])
        minus_half = sb("minus_half", [P, 1])
        weight = sb("weight", [P, 3, B])
        slot_row = sb("slot_row", [P, TOPK, B], I32)
        slot_token = sb("slot_token", [P, NT], I32)
        tokens_now = sb("tokens_now", [P, RING], I32)
        tile_expert = sb("tile_expert", [P, NT], I32)
        silu_c = sb("silu_c", [P, 2, I])
        hid = sb("hid", [P, 2, I])
        hidT = sb("hidT", [P, 2, P])

        wc = ws_down[:, 0:HG, :]
        wc_high = nc.alloc_sbuf_tensor_at("wc_high", [P, HG, D], F32R, offset=shared_at)
        wc_low = nc.alloc_sbuf_tensor_at("wc_low", [P, HG, D], F32R, offset=experts_at)
        oT_parts = nc.alloc_sbuf_tensor_at("oT_parts", [P, 2, 2, D], F32R, offset=experts_at + HG * D * 4)

        probsT_high = nc.alloc_sbuf_tensor_at("probsT_high", [P, NG, D], F32R, offset=experts_at + 2 * HG * D * 4)
        probsT_low = nc.alloc_sbuf_tensor_at("probsT_low", [P, NG, D], F32R, offset=gathered_at)
        v_parts = nc.alloc_sbuf_tensor_at("v_parts", [P, 2, 2, NG * (P + HD)], F32R, offset=experts_at + 3 * HG * D * 4)

        used = [3 * HG * D + 4 * NG * (P + HD)]

        def own(n, dt=F32):
            a = experts[:, used[0]:used[0] + n]
            used[0] += n
            return a if dt == F32 else a.bitcast(dt)

        qT = own(2 * D).rearrange("p (u n) -> p u n", u=2)
        ctxs = own(2 * P).rearrange("p (u n) -> p u n", u=2)
        k_diag = own(NG * HG * P)
        probs = own(H * P)
        xn2 = own(2 * D).rearrange("p (u n) -> p u n", u=2)
        bias_out = own(D)
        neg_max = own(H)
        row_sum = own(H)
        inv_sum = own(H)
        stats1, stats2 = own(6), own(6)
        mean1, mean2 = own(2), own(2)
        var1, var2 = own(1), own(1)
        rstd1, rstd2 = own(2), own(2)
        assert used[0] <= E * DC * 2 * I
        used[0] = E * DC * 2 * I
        logitsT = own(B * P)
        logits = own(B * (E + 1)).rearrange("p (b e) -> p b e", b=B)
        top8 = own(B * 8).rearrange("p (b n) -> p b n", b=B)
        top8_at = own(B * 8, U32).rearrange("p (b n) -> p b n", b=B)
        expert_of = own(TOPK * B).rearrange("p (k b) -> p k b", k=TOPK)
        iota_e = own(E)
        iota_t = own(NT)
        tri_e = own(E * E)
        picked = own(TOPK * B * E).rearrange("p (k n) -> p k n", k=TOPK)
        picked_any = own(B * E // 2, BF16)
        count_e, tiles_e, start_e, end_e = own(E), own(E), own(E), own(E)
        tiles_int = own(E, I32)
        before = own(E * E)
        full_tiles = own(B * E)
        full_int = own(B * E, I32)
        place = own(B * E)
        place_k = own(TOPK * B * E).rearrange("p (k n) -> p k n", k=TOPK)
        slot_f = own(TOPK * B).rearrange("p (k b) -> p k b", k=TOPK)
        tile_f = own(TOPK * B).rearrange("p (k b) -> p k b", k=TOPK)
        row_f = own(TOPK * B).rearrange("p (k b) -> p k b", k=TOPK)
        iota_p = own(P)
        own_p = own(1)
        slot_hot = logitsT.bitcast(BF16).rearrange("p (n s) -> p n s", n=TOPK * B)
        tile_hot_f32 = own(3 * D)
        tile_hot = tile_hot_f32[:, 0:TOPK * B * NT].bitcast(BF16).rearrange("p (n w t) -> p n w t", n=TOPK * B, w=2)
        xn = tile_hot_f32[:, 0:2 * D].rearrange("p (u n) -> p u n", u=2)
        probsT_full = tile_hot_f32[:, 2 * D:3 * D]
        token_f = own(NT)
        passed = own(NT * E)
        expert_f = own(NT)
        gap = own(2 * B)
        assert used[0] <= E * (DC * 2 * I + D)
        hidT_s = shared[:, :].rearrange("p (i n) -> p i n", i=IC)
        xgT = shared[:, 0:2 * D].rearrange("p (u n) -> p u n", u=2)
        y_sb = shared[:, 2 * D:4 * D].rearrange("p (u n) -> p u n", u=2)
        y_back = experts[:, E * DC * 2 * I:][:, 0:B // 2 * TOPK * D].rearrange("p (n k d) -> p n k d", k=TOPK, d=D)
        ws_parts = nc.alloc_sbuf_tensor_at("ws_parts", [P, 3, 2, DC, IS], F32R, offset=experts_at)
        x_parts = nc.alloc_sbuf_tensor_at("x_parts", [P, 2, DC, MACRO], F32R, offset=experts_at + 3 * 2 * DC * IS * 4)
        hidT_parts = nc.alloc_sbuf_tensor_at("hidT_parts", [P, 2, 2, MACRO], F32R, offset=gathered_at)

        bank = [stack.enter_context(nc.psum_tensor(f"bank{i}", [P, 512], F32)) for i in range(8)]
        turn = [bank[4], bank[5]]
        out_bank, wc_bank = bank[6], bank[7]
        gate_banks, up_banks, down_banks = bank[0:2], bank[5:7], (bank[4], bank[7], bank[2], bank[3])

        loaded = sem("loaded")
        wc_loaded = sem("wc_loaded")
        shared_loaded = sem("shared_loaded")
        x_loaded = sem("x_loaded")
        ctx_loaded = sem("ctx_loaded")
        w13_loaded = sem("w13_loaded")
        w2_loaded = sem("w2_loaded")
        consts = sem("consts")
        consts_p = sem("consts_p")
        gates_tanh = sem("gates_tanh")
        bias_scaled = sem("bias_scaled")
        st1, mv1, ve1, rs1, xn1 = (sem(n) for n in ("st1", "mv1", "ve1", "rs1", "xn1"))
        st2, mv2, ve2, rs2, xn2s = (sem(n) for n in ("st2", "mv2", "ve2", "rs2", "xn2s"))
        xb_done = sem("xb_done")
        keys_loaded = sem("keys_loaded")
        v_high, v_padded = sem("v_high"), sem("v_padded")
        xT_done, qT_saved = sem("xT_done"), sem("qT_saved")
        scored, maxed, exped, inverted, normed = (sem(n) for n in ("scored", "maxed", "exped", "inverted", "normed"))
        pT_done = sem("pT_done")
        pT_high = [sem(f"pT_high{g}") for g in range(NG)]
        pT_low = [sem(f"pT_low{g}") for g in range(NG)]
        pT_full = {g: sem(f"pT_full{g}") for g in (1, 2)}
        pv_done, oT_high, oT_low = sem("pv_done"), sem("oT_high"), sem("oT_low")
        wc_highs, wc_lows = sem("wc_highs"), sem("wc_lows")
        k_zeroed, probs_zeroed, pads_zeroed = sem("k_zeroed"), sem("probs_zeroed"), sem("pads_zeroed")
        wc_done, x1_done = sem("wc_done"), sem("x1_done")
        x2T_done, x2T_saved = sem("x2T_done"), sem("x2T_saved")
        logits_done, logits_saved, logits_turned = (sem(n) for n in ("logits_done", "logits_saved", "logits_turned"))
        xn2_stored = sem("xn2_stored")
        hots_done, slots_done, tokens_done = sem("hots_done"), sem("slots_done"), sem("tokens_done")
        picked_done, ranked = sem("picked_done"), sem("ranked")
        route = sem("route")
        gap_done, gap_exped = sem("gap_done"), sem("gap_exped")
        rows_done, experts_done = sem("rows_done"), sem("experts_done")
        down_tile_done = sem("down_tile_done")
        sg_done, su_done, silu_s_done, hidT_s_done, down_s_done, x1s_done = (
            sem(n) for n in ("sg_done", "su_done", "silu_s_done", "hidT_s_done", "down_s_done", "x1s_done"))
        ws_high, ws_low, x_high, x_low, hidT_high, hidT_low = (
            sem(n) for n in ("ws_high", "ws_low", "x_high", "x_low", "hidT_high", "hidT_low"))
        fetched = [sem(f"fetched{n}") for n in range(RING)]
        tokens_copied = sem("tokens_copied")
        xgT_done, xgT_saved, up_done, silu_done, hid_done = (
            sem(n) for n in ("xgT_done", "xgT_saved", "up_done", "silu_done", "hid_done"))
        hidT_done, hidT_saved, y_done, y_saved = (sem(n) for n in ("hidT_done", "hidT_saved", "y_done", "y_saved"))
        y_stored = [sem(f"y_stored{n}") for n in range(2)]
        y_fetched = [sem(f"y_fetched{n}") for n in range(B // 2)]
        added1, added2 = sem("added1"), sem("added2")
        out_stored = sem("out_stored")

        waited = {eng.engine: sem(f"waited_{n}")
                  for n, eng in (("sp", nc.sync), ("pool", nc.gpsimd), ("pe", nc.tensor), ("dve", nc.vector))}

        block = stack.enter_context(nc.Block())

        def apart(eng):
            eng.sem_inc(waited[eng.engine], 1)

        def batch_steps(eng, step):
            for i in range(LAG + 1):
                step(i, i % 2)
            with eng.Fori(0, (B - LAG - 3) // 2) as k:
                for u in range(2):
                    step(k * 2 + (LAG + 1 + u), u)
            for i in range(B - 2, B + LAG):
                step(i, i % 2)

        def has(i, back):
            return 0 <= i - back < B if isinstance(i, int) else True

        def tile_steps(eng, step, last=NT + 2):
            turns = NT // (2 * RING)
            for t in range(RING):
                step(t, t, 0)
            with eng.Fori(0, turns) as k:
                for n in range(2 * RING):
                    step(k * (2 * RING) + (RING + n), n % RING, k * 2 + (1 + n // RING))
            for t in range(RING * (2 * turns + 1), last):
                step(t, t % RING, t // RING)

        def tile_has(t, back):
            return 0 <= t - back < NT if isinstance(t, int) else True

        @block.sync
        def _(sp):
            def load_batch(b, u):
                need(sp, x_loaded, b * 16)
                apart(sp)
                sp.dma_start(xs[:, bass.ds(b, 1), :],
                             x_tiles[bass.ds(b, 1)].rearrange("a p d -> p a d")).then_inc(x_loaded, 16)
                need(sp, ctx_loaded, b * 16)
                apart(sp)
                need(sp, v_padded, b - 1)
                apart(sp)
                sp.dma_start(ctxs[:, u:u + 1, :],
                             ctx_tiles[bass.ds(b, 1)].rearrange("a p d -> p a d")).then_inc(ctx_loaded, 16)

            def load_keys(b):
                need(sp, scored, b * NG)
                apart(sp)
                kd = k_diag.rearrange("p (g j t) -> p g j t", g=NG, j=HG)
                for j in range(HG):
                    sp.dma_start(kd[j * HD:(j + 1) * HD, :, j, :].rearrange("p g t -> p g t"),
                                 key_tiles[bass.ds(b, 1)].rearrange("a d (g t) -> (a d) g t", g=NG)).then_inc(keys_loaded, 16)

            def store_xn2(b, u):
                need(sp, xn2s, b + 1)
                apart(sp)
                need(sp, xn2_stored, b * 16)
                apart(sp)
                sp.dma_start(xn_tiles[bass.ds(b, 1)].rearrange("a p d -> p a d"),
                             xn2[:, u:u + 1, :]).then_inc(xn2_stored, 16)

            def step(i, u):
                if has(i, 0) and not (isinstance(i, int) and i == 0):
                    load_keys(i)
                if has(i, -2):
                    load_batch(i + 2, u)
                if has(i, 3):
                    store_xn2(i - 3, 1 - u)

            load_batch(0, 0)
            sp.dma_start(wc, wc_t.rearrange("(j p) n -> p j n", p=P)).then_inc(wc_loaded, 16)
            with nc.allow_non_contiguous_dma(reason="the gates"):
                sp.dma_start(tanh_g[:, 0:1], g_xattn.rearrange("(a o) -> a o", a=1).to_broadcast([P, 1])).then_inc(loaded, 16)
                sp.dma_start(tanh_g[:, 1:2], g_ffn.rearrange("(a o) -> a o", a=1).to_broadcast([P, 1])).then_inc(loaded, 16)
                sp.dma_start(bias_out, bc.rearrange("(a o) -> a o", a=1).to_broadcast([P, D])).then_inc(loaded, 16)
                sp.dma_start(gates[:, :, 0:E], gate_t.rearrange("(c p) e -> p c e", p=P)).then_inc(loaded, 16)
                sp.dma_start(gates[:, :, E:E + 1], sgate_t.rearrange("(c p) e -> p c e", p=P)).then_inc(loaded, 16)
            sp.wait_ge(k_zeroed, 1)
            load_keys(0)
            load_batch(1, 1)

            def step_then_load(i, u):
                step(i, u)
                if isinstance(i, int) and i == LAG:
                    sp.dma_start(ws_gate[:, :, :], wsg_t.rearrange("(c p) n -> p c n", p=P)).then_inc(shared_loaded, 16)
                    sp.dma_start(ws_up[:, :, :], wsu_t.rearrange("(c p) n -> p c n", p=P)).then_inc(shared_loaded, 16)
                    sp.wait_ge(wc_lows, 1)
                    sp.dma_start(ws_down[:, :, :], wsd_t.rearrange("(c p) n -> p c n", p=P)).then_inc(shared_loaded, 16)

            batch_steps(sp, step_then_load)
            sp.wait_ge(logits_turned, 1)
            sp.wait_ge(xn2_stored, 16 * B)
            sp.dma_start(experts[:, 0:E * DC * 2 * I], w13_t).then_inc(w13_loaded, 16)
            sp.wait_ge(experts_done, 1)
            sp.dma_start(experts[:, E * DC * 2 * I:], w2_t).then_inc(w2_loaded, 16)

            def store_y(t, n, r):
                need(sp, y_saved, t + 1)
                apart(sp)
                sp.dma_start(y_slots[bass.ds(t, 1)].rearrange("a p d -> p a d"),
                             y_sb[:, n % 2:n % 2 + 1, :]).then_inc(y_stored[n % 2], 16)

            tile_steps(sp, store_y, NT)
            for b in range(B):
                sp.wait_ge(added2, b + 1)
                sp.wait_ge(x1s_done, b + 1)
                sp.dma_start(out_tiles[b], xs[:, b, :]).then_inc(out_stored, 16)
            sp.wait_ge(out_stored, 16 * B)

        @block.gpsimd
        def _(pool):
            pool.memset(minus_half[:, :], -0.5)
            pool.memset(ident[:, :], 0.0)
            pool.memset(ones_bf[:, :], 1.0)
            pool.memset(tri_e, 1.0).then_inc(consts, 1)
            pool.wait_ge(consts, 1)
            pool.affine_select(out=ident[:, :], in_=ident[:, :], compare_op=ALU.not_equal, fill=1.0, base=0,
                               pattern=[[-1, P]], channel_multiplier=1).then_inc(consts_p, 1)
            pool.affine_select(out=strict_upper[:, :], in_=ones_bf[:, :], compare_op=ALU.is_gt, fill=0.0, base=0,
                               pattern=[[1, P]], channel_multiplier=-1).then_inc(consts_p, 1)

            def inverse_root(out_, in_, started, done, b):
                need(pool, started, b + 1)
                pool.tensor_tensor(out_, in_, minus_half[:, :], ALU.pow).then_inc(done, 1)

            def norm(b, g):
                need(pool, inverted, b * NG + g + 1)
                p4 = probs[:, g * D:(g + 1) * D].rearrange("p (j t) -> p j t", j=HG)
                s4 = inv_sum[:, g * HG:(g + 1) * HG].unsqueeze(2).to_broadcast([P, HG, P])
                pool.tensor_tensor(p4, p4, s4, ALU.mult).then_inc(normed, 1)

            def pad_values(b, u):
                need(pool, ctx_loaded, b * 16 + 16)
                need(pool, pv_done, b - 1)
                apart(pool)
                values = ctxs[:, u, :].rearrange("p (g d) -> p g d", g=NG)
                padded = v_parts[:, u, :, :].rearrange("p w (g c) -> p w g c", g=NG)[:, :, :, 0:HD]
                pool.tensor_copy(padded[:, 0], values).then_inc(v_high, 1)
                need(pool, v_high, b + 1)
                pool.tensor_tensor(padded[:, 1], values, padded[:, 0].bitcast(F32), ALU.subtract).then_inc(v_padded, 1)

            def low_of_pT(b, g):
                need(pool, pT_full[g], b + 1)
                need(pool, pv_done, b)
                pool.tensor_tensor(probsT_low[:, g, :], probsT_full, probsT_high[:, g, :].bitcast(F32),
                                   ALU.subtract).then_inc(pT_low[g], 1)

            def add_bias(b):
                need(pool, xn1, b + 1)
                pool.tensor_tensor(xs[:, bass.ds(b, 1), :], xs[:, bass.ds(b, 1), :],
                                   bias_out.unsqueeze(1), ALU.add).then_inc(xb_done, 1)

            inverse_root(rstd1[:, 0:1], var1, ve1, rs1, 0)
            pool.wait_ge(pads_zeroed, 1)
            tri = tri_e.rearrange("p (a b) -> p a b", a=E)
            pool.affine_select(out=tri, in_=tri, compare_op=ALU.is_gt, fill=0.0, base=0,
                               pattern=[[1, E], [-1, E]], channel_multiplier=0).then_inc(consts_p, 1)
            pool.iota(iota_e, [[1, E]], base=0, channel_multiplier=0, allow_small_or_imprecise_dtypes=True).then_inc(consts_p, 1)
            pool.iota(iota_t, [[1, NT]], base=0, channel_multiplier=0, allow_small_or_imprecise_dtypes=True).then_inc(consts_p, 1)
            pool.iota(iota_p, [[1, P]], base=0, channel_multiplier=0, allow_small_or_imprecise_dtypes=True).then_inc(consts_p, 1)
            pool.iota(own_p, [[0, 1]], base=0, channel_multiplier=1, allow_small_or_imprecise_dtypes=True).then_inc(consts_p, 1)
            pool.wait_ge(bias_scaled, 1)

            def step(i, u):
                if has(i, 2):
                    low_of_pT(i - 2, 2)
                if has(i, 1):
                    norm(i - 1, 0)
                    norm(i - 1, 1)
                if has(i, 0):
                    pad_values(i, u)
                    add_bias(i)
                if has(i, 1):
                    norm(i - 1, 2)
                    norm(i - 1, 3)
                    low_of_pT(i - 1, 1)
                if has(i, 2):
                    inverse_root(rstd2[:, 0:1], var2, ve2, rs2, i - 2)
                if has(i, -1):
                    inverse_root(rstd1[:, 0:1], var1, ve1, rs1, i + 1)

            batch_steps(pool, step)

            pool.wait_ge(tokens_done, 1)
            pool.wait_ge(xn2_stored, 16 * B)

            def fetch(t, n, r):
                need(pool, xgT_done, t - RING + 1)
                pool.tensor_copy(tokens_now[:, n:n + 1], slot_token[:, bass.ds(t, 1)]).then_inc(tokens_copied, 1)
                need(pool, tokens_copied, t + 1)
                apart(pool)
                pool.indirect_dma_start(
                    gathered[:, n, :], None, xn_dram,
                    bass.IndirectOffsetOnAxis(ap=tokens_now[:, n:n + 1].bitcast(U32), axis=0)).then_inc(fetched[n], 16)

            tile_steps(pool, fetch, NT)
            pool.wait_ge(rows_done, 1)
            for n in range(2):
                pool.wait_ge(y_stored[n], 16 * ((NT + 1 - n) // 2))
            for b in range(B):
                n = b % (B // 2)
                if b >= B // 2:
                    pool.wait_ge(added2, n + 1)
                for k in range(TOPK):
                    pool.indirect_dma_start(
                        y_back[:, n, k, :], None, y_dram,
                        bass.IndirectOffsetOnAxis(ap=slot_row[:, k, b:b + 1].bitcast(U32), axis=0)).then_inc(y_fetched[n], 16)

        @block.tensor
        def _(pe):
            def four_transposes(dst, src):
                for c in range(4):
                    last = pe.transpose(dst[:, c * P:(c + 1) * P], src[:, c * P:(c + 1) * P], ident[:, :])
                return last

            def x_transpose(i, u):
                need(pe, xn1, i + 1)
                need(pe, pT_low[3], i - 1)
                if isinstance(i, int) and i == 1:
                    need(pe, qT_saved, 1)
                four_transposes(turn[0], xn[:, u, :]).then_inc(xT_done, 1)

            def project(b, u, half):
                if half == 0:
                    need(pe, oT_high, b + 1)
                    need(pe, x1_done, b)
                    for j in range(HG):
                        for w in (wc_high, wc_low):
                            pe.matmul(wc_bank[:, :], oT_parts[:, u, 0, j * P:(j + 1) * P], w[:, j, :],
                                      start=(j == 0 and w is wc_high), stop=False)
                else:
                    need(pe, oT_low, b + 1)
                    for j in range(HG):
                        mm = pe.matmul(wc_bank[:, :], oT_parts[:, u, 1, j * P:(j + 1) * P], wc_high[:, j, :],
                                       start=False, stop=(j == HG - 1))
                    mm.then_inc(wc_done, 1)

            def x2_transpose(b, i, u):
                need(pe, xn2s, b + 1)
                if has(i, 0):
                    need(pe, qT_saved, i + 1)
                else:
                    need(pe, pT_low[3], min(i - 1, B))
                    need(pe, x2T_saved, b)
                four_transposes(turn[0], xn2[:, u, :]).then_inc(x2T_done, 1)

            def p_transpose(b, g):
                need(pe, normed, b * NG + g + 1)
                four_transposes(turn[1 - g % 2], probs[:, g * D:(g + 1) * D]).then_inc(pT_done, 1)

            def pv_high(b, g, u):
                need(pe, pT_high[g], b + 1)
                if g == 0:
                    need(pe, v_padded, b + 1)
                    need(pe, oT_low, b)
                for part in range(2):
                    pe.matmul(out_bank[:, :], v_parts[:, u, part, g * P:(g + 1) * P], probsT_high[:, g, :],
                              start=(g == 0 and part == 0), stop=False)

            def pv_low(b, g, u):
                need(pe, pT_low[g], b + 1)
                mm = pe.matmul(out_bank[:, :], v_parts[:, u, 0, g * P:(g + 1) * P], probsT_low[:, g, :],
                               start=False, stop=(g == NG - 1))
                if g == NG - 1:
                    mm.then_inc(pv_done, 1)

            def router(b, i):
                need(pe, x2T_saved, b + 1)
                need(pe, exped, NG * (min(i, B) if isinstance(i, int) else i) - 1)
                need(pe, logits_saved, b)
                for c in range(DC):
                    mm = pe.matmul(bank[2][0:E + 1, 0:P], gates[:, c, :], xnT[:, c, bass.ds(b * P, P)],
                                   start=(c == 0), stop=(c == DC - 1))
                mm.then_inc(logits_done, 1)

            def scores(i, u, groups):
                need(pe, qT_saved, i + 1)
                need(pe, keys_loaded, i * (16 * HG) + 16 * HG)
                for g in groups:
                    need(pe, exped, i * NG + g + 1 - NG)
                    if g == 2:
                        need(pe, logits_saved, i - LAG + 1)
                    pe.matmul(bank[g][:, :], qT[:, u, g * P:(g + 1) * P], k_diag[:, g * D:(g + 1) * D],
                              start=True, stop=True).then_inc(scored, 1)

            def step(i, u):
                v = 1 - u
                if has(i, 0):
                    x_transpose(i, u)
                if has(i, 1):
                    scores(i - 1, v, (3,))
                if has(i, 2):
                    if isinstance(i, int) and i == 2:
                        pe.wait_ge(wc_highs, 1)
                        pe.wait_ge(wc_lows, 1)
                    project(i - 2, u, 0)
                if has(i, 3):
                    x2_transpose(i - 3, i, v)
                if has(i, 2):
                    project(i - 2, u, 1)
                if has(i, 1):
                    b = i - 1
                    need(pe, pT_full[2], i - 1)
                    p_transpose(b, 0)
                    if has(i, 3):
                        need(pe, x2T_saved, i - 2)
                    else:
                        need(pe, qT_saved, i + 1)
                    p_transpose(b, 1)
                if has(i, 3):
                    if isinstance(i, int) and i == 3:
                        pe.wait_ge(loaded, 16 * 5)
                    router(i - 3, i)
                if has(i, 1):
                    pv_high(i - 1, 0, v)
                    pv_low(i - 1, 0, v)
                if has(i, 0):
                    scores(i, u, (0,))
                if has(i, 1):
                    p_transpose(b, 2)
                if has(i, 0):
                    scores(i, u, (1,))
                if has(i, 1):
                    need(pe, pT_full[1], b + 1)
                    p_transpose(b, 3)
                if has(i, 0):
                    scores(i, u, (2,))
                if has(i, 1):
                    pv_high(b, 1, v)
                    pv_low(b, 1, v)
                    pv_high(b, 2, v)
                    pv_high(b, 3, v)
                    pv_low(b, 2, v)
                    pv_low(b, 3, v)

            pe.wait_ge(consts_p, 2)

            def shared_gate(m, ic):
                need(pe, silu_s_done, m * IC + ic - 1)
                for c in range(DC):
                    mm = pe.matmul(gate_banks[ic % 2][:, :], ws_gate[:, c, ic * P:(ic + 1) * P],
                                   xnT[:, c, bass.ds(m * MACRO, MACRO)], start=(c == 0), stop=(c == DC - 1))
                mm.then_inc(sg_done, 1)

            def shared_up(m, ic):
                need(pe, hidT_s_done, m * IC + ic - 1)
                for c in range(DC):
                    mm = pe.matmul(up_banks[ic % 2][:, :], ws_up[:, c, ic * P:(ic + 1) * P],
                                   xnT[:, c, bass.ds(m * MACRO, MACRO)], start=(c == 0), stop=(c == DC - 1))
                mm.then_inc(su_done, 1)

            def shared_down(m, ic):
                need(pe, hidT_s_done, m * IC + ic + 1)
                for tt in range(TM):
                    if ic == 0:
                        need(pe, x1s_done, m * TM + tt + 1 - TM)
                    mm = pe.matmul(down_banks[tt][:, :], hidT_s[:, ic, tt * P:(tt + 1) * P], ws_down[:, ic, :],
                                   start=(ic == 0), stop=(ic == IC - 1))
                mm.then_inc(down_s_done, 1)

            def step_then_gate(i, u):
                step(i, u)
                if isinstance(i, int) and i == B + LAG - 2:
                    pe.wait_ge(shared_loaded, 16 * 3)
                    shared_gate(0, 0)

            batch_steps(pe, step_then_gate)

            need(pe, logits_saved, B)
            for b in range(B):
                last = pe.transpose(bank[2][:, b * (E + 1):(b + 1) * (E + 1)],
                                    logitsT[0:E + 1, b * P:(b + 1) * P], ident[0:E + 1, 0:E + 1])
            last.then_inc(logits_turned, 1)
            shared_up(0, 0)

            pe.wait_ge(picked_done, 1)
            pe.matmul(bank[3][:, 0:B * E], strict_upper[:, :], picked_any, start=True, stop=False, skip_group_check=True)
            for b in range(B - 1):
                left = B - 1 - b
                one = picked_any[:, b * E:(b + 1) * E].unsqueeze(1).to_broadcast([P, left, E])
                pe.matmul(bank[3][:, (b + 1) * E:B * E].rearrange("p (b e) -> p b e", e=E), ones_bf[:, :], one,
                          start=False, stop=(b == B - 2), skip_group_check=True)
            pe.matmul(bank[4][:, 0:B * E], ones_bf[:, :], picked_any, start=True, stop=True).then_inc(ranked, 1)
            for ic in range(1, 3):
                shared_gate(0, ic)
                shared_up(0, ic)
            shared_gate(0, 3)

            pe.wait_ge(hots_done, 1)
            for n in range(TOPK * B):
                mm = pe.matmul(bank[2][:, 0:2 * NT], slot_hot[:, n, :], tile_hot[:, n, :, :].rearrange("p w t -> p (w t)"),
                               start=(n == 0), stop=(n == TOPK * B - 1))
            mm.then_inc(slots_done, 1)
            shared_up(0, 3)
            pe.wait_ge(tokens_done, 1)
            for ic in range(IC):
                shared_down(0, ic)

            pe.wait_ge(w13_loaded, 16)
            pe.wait_ge(w2_loaded, 16)

            def expert_of_tile(t):
                return pe.value_load(tile_expert[0:1, bass.ds(t, 1)], min_val=0, max_val=E - 1)

            def tile_step(t, n, r):
                u, v = n % 2, 1 - n % 2
                if tile_has(t, 2):
                    e_down = expert_of_tile(t - 2)
                if tile_has(t, 1):
                    e_up = expert_of_tile(t - 1)
                if tile_has(t, 2):
                    need(pe, hid_done, t - 1)
                    need(pe, hidT_saved, t - 3)
                    if isinstance(t, int) and t == 3:
                        need(pe, x1s_done, 2)
                    pe.transpose(bank[6 + u][:, 0:P], hid[:, u, :], ident[:, :]).then_inc(hidT_done, 1)
                if tile_has(t, 1):
                    need(pe, xgT_saved, t)
                    need(pe, hid_done, t - 2)
                    if isinstance(t, int) and t == 1:
                        need(pe, x1s_done, 1)
                    for c in range(DC):
                        mm = pe.matmul(bank[4 + v][:, 0:2 * I], xgT[:, v, c * P:(c + 1) * P],
                                       w13[:, bass.ds(e_up * DC + c, 1), :], start=(c == 0), stop=(c == DC - 1))
                    mm.then_inc(up_done, 1)
                if tile_has(t, 0):
                    need(pe, fetched[n], r * 16 + 16)
                    need(pe, xgT_saved, t - 1)
                    four_transposes(bank[u], gathered[:, n, :]).then_inc(xgT_done, 1)
                if isinstance(t, int) and t == NT + 1:
                    shared_gate(1, 0)
                if tile_has(t, 2):
                    need(pe, hidT_saved, t - 1)
                    need(pe, y_saved, t - 3)
                    if isinstance(t, int) and t < 4:
                        need(pe, x1s_done, t + 1)
                    pe.matmul(bank[2 + u][:, :], hidT[:, u, :], w2[:, bass.ds(e_down, 1), :],
                              start=True, stop=True).then_inc(y_done, 1)

            tile_steps(pe, tile_step)
            shared_up(1, 0)
            pe.wait_ge(y_saved, NT)

            def in_parts(into, left, right, first, last):
                for l, r in ((0, 0), (1, 0), (0, 1)):
                    mm = pe.matmul(into, left(l), right(r), start=(first and (l, r) == (0, 0)), stop=(last and r == 1))
                return mm

            def parts_first(m, ic, w, into, done):
                if isinstance(m, int) and m == 1:
                    need(pe, ws_high, SPLIT_ORDER.index(ic) * 3 + w + 1)
                    need(pe, ws_low, SPLIT_ORDER.index(ic) * 3 + w + 1)
                for c in range(DC):
                    if w == 0 and ic == (1 if isinstance(m, int) and m == 1 else 0):
                        need(pe, x_high, m * DC + (c + 1 - DC))
                        need(pe, x_low, m * DC + (c + 1 - DC))
                    mm = in_parts(into, lambda part: ws_parts[:, w, part, c, ic * P:(ic + 1) * P],
                                  lambda part: x_parts[:, part, c, :], c == 0, c == DC - 1)
                mm.then_inc(done, 1)

            def parts_down(m, ic):
                if isinstance(m, int) and m == 1:
                    need(pe, ws_high, SPLIT_ORDER.index(ic) * 3 + 3)
                    need(pe, ws_low, SPLIT_ORDER.index(ic) * 3 + 3)
                need(pe, hidT_high, m * IC + (ic + 1 - IC))
                need(pe, hidT_low, m * IC + (ic + 1 - IC))
                for tt in range(TM):
                    if ic == 0:
                        need(pe, x1s_done, m * TM + tt + 1 - TM)
                    mm = in_parts(down_banks[tt][:, :], lambda part: hidT_parts[:, ic % 2, part, tt * P:(tt + 1) * P],
                                  lambda part: ws_parts[:, 2, part, ic, :], ic == 0, ic == IC - 1)
                    if ic == IC - 1 and tt < TM - 1:
                        mm.then_inc(down_tile_done, 1)
                mm.then_inc(down_s_done, 1)

            def macro_in_parts(m):
                for ic in range(IC):
                    if isinstance(m, int) and m == 1 and ic == 0:
                        continue
                    need(pe, silu_s_done, m * IC + ic - 1)
                    parts_first(m, ic, 0, gate_banks[ic % 2][:, :], sg_done)
                    need(pe, hidT_s_done, m * IC + ic - 1)
                    parts_first(m, ic, 1, up_banks[ic % 2][:, :], su_done)
                    if 0 < ic < IC - 1:
                        parts_down(m, ic - 1)
                parts_down(m, IC - 2)
                parts_down(m, IC - 1)

            macro_in_parts(1)
            with pe.Fori(2, NM) as m:
                macro_in_parts(m)

        @block.scalar
        def _(act):
            act.wait_ge(probs_zeroed, 1)
            for u in range(2):
                for part in range(2):
                    last = nc.scalar.activation(v_parts[:, u, part, :], probs[:, 0:NG * (P + HD)], ACT.Copy)
            last.then_inc(pads_zeroed, 1)
            act.wait_ge(pads_zeroed, 1)

            def exps(b, g):
                need(act, maxed, b * NG + g + 1)
                need(act, pT_done, b * NG + g + 1 - NG)
                for j in range(HG):
                    h = g * HG + j
                    last = nc.scalar.activation(probs[:, h * P:(h + 1) * P], bank[g][:, j * P:(j + 1) * P], ACT.Exp,
                                                bias=neg_max[:, h:h + 1], accum_out=row_sum[:, h:h + 1])
                last.then_inc(exped, 1)

            def save_x2T(b):
                need(act, x2T_done, b + 1)
                nc.scalar.activation(xnT[:, :, bass.ds(b * P, P)], turn[0][:, :].rearrange("p (c n) -> p c n", c=DC),
                                     ACT.Copy).then_inc(x2T_saved, 1)

            def save_pT(b, g):
                need(act, pT_done, b * NG + g + 1)
                need(act, pv_done, b)
                nc.scalar.activation(probsT_high[:, g, :], turn[1 - g % 2][:, :], ACT.Copy).then_inc(pT_high[g], 1)
                if g in (1, 2):
                    need(act, pT_low[3 - g], b if g == 1 else b + 1)
                    nc.scalar.activation(probsT_full, turn[1 - g % 2][:, :], ACT.Copy).then_inc(pT_full[g], 1)

            def step(i, u):
                if has(i, 2):
                    save_pT(i - 2, 2)
                    save_pT(i - 2, 3)
                if has(i, 1):
                    exps(i - 1, 0)
                    exps(i - 1, 1)
                if has(i, 0):
                    need(act, xT_done, i + 1)
                    nc.scalar.activation(qT[:, u, :], turn[0][:, :], ACT.Copy).then_inc(qT_saved, 1)
                if has(i, 1):
                    exps(i - 1, 2)
                if has(i, 3):
                    save_x2T(i - 3)
                if has(i, 1):
                    exps(i - 1, 3)
                    save_pT(i - 1, 1)

            act.wait_ge(wc_loaded, 16)
            nc.scalar.activation(wc_high[:, :, :], wc, ACT.Copy).then_inc(wc_highs, 1)

            def step_then_tanh(i, u):
                step(i, u)
                if isinstance(i, int) and i == 0:
                    act.wait_ge(loaded, 16 * 5)
                    nc.scalar.activation(tanh_g[:, :], tanh_g[:, :], ACT.Tanh).then_inc(gates_tanh, 1)

            batch_steps(act, step_then_tanh)

            def silu_shared(m, ic):
                need(act, sg_done, m * IC + ic + 1)
                need(act, down_s_done, m * IC + ic + 1 - IC)
                nc.scalar.activation(hidT_s[:, ic, :], gate_banks[ic % 2][:, :], ACT.Silu).then_inc(silu_s_done, 1)

            silu_shared(0, 0)
            act.wait_ge(gap_done, 1)
            nc.scalar.activation(gap, gap, ACT.Exp).then_inc(gap_exped, 1)
            for ic in range(1, IC):
                silu_shared(0, ic)

            def tile_step(t, n, r):
                u, v = n % 2, 1 - n % 2
                if tile_has(t, 1):
                    need(act, up_done, t)
                    need(act, hid_done, t - 2)
                    nc.scalar.activation(silu_c[:, v, :], bank[4 + v][:, 0:I], ACT.Silu).then_inc(silu_done, 1)
                if tile_has(t, 0):
                    need(act, xgT_done, t + 1)
                    need(act, up_done, t - 1)
                    nc.scalar.activation(xgT[:, u, :], bank[u][:, :], ACT.Copy).then_inc(xgT_saved, 1)

            tile_steps(act, tile_step)

            def high_of_weights(ic):
                for w, weights in enumerate((ws_gate, ws_up, ws_down)):
                    at = (slice(ic, ic + 1), slice(0, D)) if w == 2 else (slice(0, DC), slice(ic * P, (ic + 1) * P))
                    nc.scalar.activation(ws_parts[:, w, 0, at[0], at[1]], weights[:, at[0], at[1]],
                                         ACT.Copy).then_inc(ws_high, 1)

            def high_of_tokens(m):
                need(act, su_done, m * IC)
                for c in range(DC):
                    nc.scalar.activation(x_parts[:, 0, c, :], xnT[:, c, bass.ds(m * MACRO, MACRO)],
                                         ACT.Copy).then_inc(x_high, 1)

            def macro_in_parts(m, more):
                for ic in range(IC):
                    need(act, sg_done, m * IC + ic + 1)
                    if isinstance(m, int) and m == 1:
                        need(act, down_s_done, IC)
                    else:
                        need(act, hidT_low, m * IC + (ic + 1 - 2 * IC))
                    nc.scalar.activation(hidT_s[:, ic, :], gate_banks[ic % 2][:, :], ACT.Silu).then_inc(silu_s_done, 1)
                    need(act, hidT_s_done, m * IC + ic + 1)
                    need(act, down_s_done, m * IC + ic - 1)
                    nc.scalar.activation(hidT_parts[:, ic % 2, 0, :], hidT_s[:, ic, :], ACT.Copy).then_inc(hidT_high, 1)
                    if isinstance(m, int) and m == 1 and ic < IC - 2:
                        high_of_weights(SPLIT_ORDER[ic + 2])
                if more:
                    high_of_tokens(m + 1)

            act.wait_ge(up_done, NT)
            high_of_tokens(1)
            high_of_weights(SPLIT_ORDER[0])
            high_of_weights(SPLIT_ORDER[1])
            macro_in_parts(1, True)
            with act.Fori(2, NM - 1) as m:
                macro_in_parts(m, True)
            macro_in_parts(NM - 1, False)

        @block.vector
        def _(dve):
            nc.vector.memset(probs[:, 0:NG * (P + HD)], 0.0).then_inc(probs_zeroed, 1)
            nc.vector.memset(k_diag, 0.0).then_inc(k_zeroed, 1)

            def x_at(b):
                return xs[:, bass.ds(b, 1), :].rearrange("p a d -> p (a d)")

            def stats_x(b):
                need(dve, x_loaded, b * 16 + 16)
                apart(dve)
                nc.vector.bn_stats(stats1, x_at(b)).then_inc(st1, 1)

            def mean_x(b):
                need(dve, st1, b + 1)
                apart(dve)
                nc.vector.bn_aggr(mean1, stats1).then_inc(mv1, 1)

            def scale_x(b):
                need(dve, mv1, b + 1)
                nc.vector.tensor_scalar(var1, mean1[:, 1:2], EPS, float(HD), ALU.add, ALU.mult).then_inc(ve1, 1)

            def norm_x(b, u):
                need(dve, rs1, b + 1)
                nc.vector.tensor_scalar(xn[:, u, :], x_at(b), mean1[:, 0:1], rstd1[:, 0:1],
                                        ALU.subtract, ALU.mult).then_inc(xn1, 1)

            def max_of(b, g):
                need(dve, scored, b * NG + g + 1)
                nc.vector.tensor_reduce(neg_max[:, g * HG:(g + 1) * HG],
                                        bank[g][:, :].rearrange("p (j t) -> p j t", j=HG), AX.X, ALU.max,
                                        negate=True).then_inc(maxed, 1)

            def invert(b, g):
                need(dve, exped, b * NG + g + 1)
                nc.vector.reciprocal(inv_sum[:, g * HG:(g + 1) * HG],
                                     row_sum[:, g * HG:(g + 1) * HG]).then_inc(inverted, 1)

            def add_attention(b):
                need(dve, wc_done, b + 1)
                need(dve, xb_done, b + 1)
                nc.vector.scalar_tensor_tensor(x_at(b), wc_bank[:, :], tanh_g[:, 0:1], x_at(b),
                                               ALU.mult, ALU.add).then_inc(x1_done, 1)

            def stats_x1(b):
                need(dve, x1_done, b + 1)
                apart(dve)
                nc.vector.bn_stats(stats2, x_at(b)).then_inc(st2, 1)

            def mean_x1(b):
                need(dve, st2, b + 1)
                apart(dve)
                nc.vector.bn_aggr(mean2, stats2).then_inc(mv2, 1)

            def scale_x1(b):
                need(dve, mv2, b + 1)
                nc.vector.tensor_scalar(var2, mean2[:, 1:2], EPS, None, ALU.add).then_inc(ve2, 1)

            def norm_x1(b, u):
                need(dve, rs2, b + 1)
                need(dve, x2T_done, b - 1)
                need(dve, xn2_stored, b * 16 - 16)
                nc.vector.tensor_scalar(xn2[:, u, :], x_at(b), mean2[:, 0:1], rstd2[:, 0:1],
                                        ALU.subtract, ALU.mult).then_inc(xn2s, 1)

            def save_pT(b, g):
                need(dve, pT_done, b * NG + g + 1)
                need(dve, pv_done, b)
                nc.vector.tensor_copy(probsT_high[:, g, :], turn[1 - g % 2][:, :]).then_inc(pT_high[g], 1)

            def low_of_pT(b, g):
                need(dve, pT_high[g], b + 1)
                need(dve, pv_done, b)
                nc.vector.tensor_tensor(probsT_low[:, g, :], turn[1 - g % 2][:, :], probsT_high[:, g, :].bitcast(F32),
                                        ALU.subtract).then_inc(pT_low[g], 1)

            def step(i, u):
                if has(i, 1):
                    max_of(i - 1, 0)
                    max_of(i - 1, 1)
                if has(i, 2):
                    low_of_pT(i - 2, 3)
                if has(i, 0):
                    norm_x(i, u)
                if has(i, 3):
                    norm_x1(i - 3, 1 - u)
                if has(i, 1):
                    invert(i - 1, 0)
                    max_of(i - 1, 2)
                if has(i, 2):
                    need(dve, pv_done, i - 1)
                    need(dve, wc_done, i - 3)
                    nc.vector.tensor_copy(oT_parts[:, u, 0, :], out_bank[:, :]).then_inc(oT_high, 1)
                if has(i, 1):
                    max_of(i - 1, 3)
                if has(i, 2):
                    need(dve, oT_high, i - 1)
                    nc.vector.tensor_tensor(oT_parts[:, u, 1, :], out_bank[:, :],
                                            oT_parts[:, u, 0, :].bitcast(F32), ALU.subtract).then_inc(oT_low, 1)
                if has(i, 1):
                    invert(i - 1, 1)
                    invert(i - 1, 2)
                if isinstance(i, int) and i == 0:
                    dve.wait_ge(wc_highs, 1)
                    nc.vector.tensor_tensor(wc_low[:, :, :], wc, wc_high[:, :, :].bitcast(F32),
                                            ALU.subtract).then_inc(wc_lows, 1)
                if has(i, -1):
                    stats_x(i + 1)
                if has(i, 1):
                    save_pT(i - 1, 0)
                if has(i, -1):
                    mean_x(i + 1)
                if has(i, 1):
                    low_of_pT(i - 1, 0)
                    invert(i - 1, 3)
                if has(i, -1):
                    scale_x(i + 1)
                if has(i, 2):
                    add_attention(i - 2)
                    stats_x1(i - 2)
                if has(i, 3):
                    need(dve, logits_done, i - 2)
                    nc.vector.tensor_copy(logitsT[0:E + 1, bass.ds((i - 3) * P, P)],
                                          bank[2][0:E + 1, 0:P]).then_inc(logits_saved, 1)
                if has(i, 2):
                    mean_x1(i - 2)
                    scale_x1(i - 2)

            stats_x(0)
            mean_x(0)
            scale_x(0)

            def step_then_bias(i, u):
                step(i, u)
                if isinstance(i, int) and i == 0:
                    dve.wait_ge(gates_tanh, 1)
                    nc.vector.tensor_scalar(bias_out, bias_out, tanh_g[:, 0:1], None, ALU.mult).then_inc(bias_scaled, 1)

            batch_steps(dve, step_then_bias)

            count = [0]

            def then(ins):
                count[0] += 1
                ins.then_inc(route, 1)
                dve.wait_ge(route, count[0])

            dve.wait_ge(logits_turned, 1)
            dve.wait_ge(consts_p, 7)
            then(nc.vector.tensor_copy(logits, bank[2][:, 0:B * (E + 1)].rearrange("p (b e) -> p b e", b=B)))
            for b in range(B):
                last = nc.vector.max(top8[:, b, :], logits[:, b, 0:E])
            then(last)
            for b in range(B):
                last = nc.vector.max_index(top8_at[:, b, :], top8[:, b, :], logits[:, b, 0:E])
            then(last)
            then(nc.vector.tensor_copy(expert_of, top8_at[:, :, 0:TOPK].rearrange("p b k -> p k b")))
            for k in range(TOPK):
                last = nc.vector.tensor_tensor(
                    picked[:, k, :].rearrange("p (b e) -> p b e", b=B),
                    expert_of[:, k, :].unsqueeze(2).to_broadcast([P, B, E]),
                    iota_e.unsqueeze(1).to_broadcast([P, B, E]), ALU.is_equal)
            then(last)
            nc.vector.tensor_tensor(picked_any, picked[:, 0, :], picked[:, 1, :], ALU.add).then_inc(picked_done, 1)
            nc.vector.tensor_tensor(gap[:, 0:B], top8[:, :, 1], top8[:, :, 0], ALU.subtract)
            nc.vector.tensor_scalar(gap[:, B:2 * B], logits[:, :, E], -1.0, None, ALU.mult).then_inc(gap_done, 1)

            def hidden_shared(m, ic):
                need(dve, silu_s_done, m * IC + ic + 1)
                need(dve, su_done, m * IC + ic + 1)
                nc.vector.tensor_tensor(hidT_s[:, ic, :], up_banks[ic % 2][:, :], hidT_s[:, ic, :],
                                        ALU.mult).then_inc(hidT_s_done, 1)

            hidden_shared(0, 0)

            dve.wait_ge(ranked, 1)
            then(nc.vector.tensor_reduce(count_e, bank[4][:, 0:B * E].rearrange("p (b e) -> p e b", b=B), AX.X, ALU.add))
            then(nc.vector.tensor_scalar(tiles_e, count_e, 1.0 / P, (P - 1.0) / P - FLOOR, ALU.mult, ALU.add))
            then(nc.vector.tensor_copy(tiles_int, tiles_e))
            then(nc.vector.tensor_copy(tiles_e, tiles_int))
            then(nc.vector.tensor_tensor(before.rearrange("p (a b) -> p a b", a=E), tri_e.rearrange("p (a b) -> p a b", a=E),
                                         tiles_e.unsqueeze(1).to_broadcast([P, E, E]), ALU.mult))
            then(nc.vector.tensor_reduce(start_e, before.rearrange("p (a b) -> p a b", a=E), AX.X, ALU.add))
            then(nc.vector.tensor_tensor(end_e, start_e, tiles_e, ALU.add))
            then(nc.vector.tensor_scalar(place, bank[3][:, 0:B * E], 1.0 / P, -FLOOR, ALU.mult, ALU.add))
            then(nc.vector.tensor_copy(full_int, place))
            then(nc.vector.tensor_copy(full_tiles, full_int))
            then(nc.vector.scalar_tensor_tensor(place, full_tiles, -1.0 * P, bank[3][:, 0:B * E], ALU.mult, ALU.add))
            then(nc.vector.tensor_tensor(full_tiles.rearrange("p (b e) -> p b e", b=B), full_tiles.rearrange("p (b e) -> p b e", b=B),
                                         start_e.unsqueeze(1).to_broadcast([P, B, E]), ALU.add))
            for table, result in ((place, slot_f), (full_tiles, tile_f)):
                then(nc.vector.tensor_tensor(place_k, picked, table.unsqueeze(1).to_broadcast([P, TOPK, B * E]), ALU.mult))
                then(nc.vector.tensor_reduce(result, place_k.rearrange("p k (b e) -> p k b e", b=B), AX.X, ALU.add))
            hidden_shared(0, 1)
            nc.vector.tensor_tensor(slot_hot, slot_f.rearrange("p k b -> p (k b)").unsqueeze(2).to_broadcast([P, TOPK * B, P]),
                                    iota_p.unsqueeze(1).to_broadcast([P, TOPK * B, P]), ALU.is_equal)
            then(nc.vector.tensor_tensor(tile_hot[:, :, 0, :], tile_f.rearrange("p k b -> p (k b)").unsqueeze(2).to_broadcast([P, TOPK * B, NT]),
                                         iota_t.unsqueeze(1).to_broadcast([P, TOPK * B, NT]), ALU.is_equal))
            for k in range(TOPK):
                last = nc.vector.tensor_tensor(tile_hot[:, k * B:(k + 1) * B, 1, :], tile_hot[:, k * B:(k + 1) * B, 0, :],
                                               iota_e[:, 0:B].unsqueeze(2).to_broadcast([P, B, NT]), ALU.mult)
            then(last)
            nc.vector.tensor_scalar(tile_hot[:, :, 0, :], tile_hot[:, :, 0, :], own_p[:, 0:1], None,
                                    ALU.mult).then_inc(hots_done, 1)
            then(nc.vector.scalar_tensor_tensor(row_f, slot_f, float(NT), tile_f, ALU.mult, ALU.add))
            nc.vector.tensor_copy(slot_row[:, :, :], row_f).then_inc(rows_done, 1)
            hidden_shared(0, 2)
            then(nc.vector.tensor_tensor(passed.rearrange("p (t e) -> p t e", e=E),
                                         end_e.unsqueeze(1).to_broadcast([P, NT, E]),
                                         iota_t.unsqueeze(2).to_broadcast([P, NT, E]), ALU.is_le))
            then(nc.vector.tensor_reduce(expert_f, passed.rearrange("p (t e) -> p t e", e=E), AX.X, ALU.add))
            then(nc.vector.tensor_scalar(expert_f, expert_f, E - 1.0, None, ALU.min))
            nc.vector.tensor_copy(tile_expert[:, :], expert_f)
            dve.wait_ge(slots_done, 1)
            then(nc.vector.tensor_copy(token_f, bank[2][:, 0:NT]))
            then(nc.vector.scalar_tensor_tensor(token_f, bank[2][:, NT:2 * NT], float(P), token_f, ALU.mult, ALU.add))
            nc.vector.tensor_copy(slot_token[:, :], token_f).then_inc(tokens_done, 1)
            dve.wait_ge(gap_exped, 1)
            then(nc.vector.tensor_scalar(place[:, 0:2 * B], gap, 1.0, None, ALU.add))
            then(nc.vector.reciprocal(full_tiles[:, 0:2 * B], place[:, 0:2 * B]))
            then(nc.vector.tensor_scalar(weight[:, 0, :], full_tiles[:, 0:B], tanh_g[:, 1:2], None, ALU.mult))
            nc.vector.tensor_scalar(weight[:, 2, :], full_tiles[:, B:2 * B], tanh_g[:, 1:2], None, ALU.mult)
            then(nc.vector.tensor_tensor(weight[:, 1, :], weight[:, 0, :], gap[:, 0:B], ALU.mult))
            nc.vector.memset(expert_f[:, 0:1], 0.0).then_inc(experts_done, 1)
            hidden_shared(0, 3)

            def add_shared(m):
                for tt in range(TM):
                    if m == 0 or tt == TM - 1:
                        need(dve, down_s_done, m * IC + IC)
                    else:
                        need(dve, down_tile_done, (m - 1) * (TM - 1) + tt + 1)
                    at = m * TM + tt
                    nc.vector.scalar_tensor_tensor(
                        x_at(at), down_banks[tt][:, :], weight[:, 2, bass.ds(at, 1)], x_at(at),
                        ALU.mult, ALU.add).then_inc(x1s_done, 1)

            add_shared(0)

            def low_of_weights(ic):
                for w, weights in enumerate((ws_gate, ws_up, ws_down)):
                    need(dve, ws_high, SPLIT_ORDER.index(ic) * 3 + w + 1)
                    at = (slice(ic, ic + 1), slice(0, D)) if w == 2 else (slice(0, DC), slice(ic * P, (ic + 1) * P))
                    nc.vector.tensor_tensor(ws_parts[:, w, 1, at[0], at[1]], weights[:, at[0], at[1]],
                                            ws_parts[:, w, 0, at[0], at[1]].bitcast(F32), ALU.subtract).then_inc(ws_low, 1)

            def low_of_tokens(m):
                for c in range(DC):
                    need(dve, x_high, (m - 1) * DC + c + 1)
                    nc.vector.tensor_tensor(x_parts[:, 1, c, :], xnT[:, c, m * MACRO:(m + 1) * MACRO],
                                            x_parts[:, 0, c, :].bitcast(F32), ALU.subtract).then_inc(x_low, 1)

            def tile_step(t, n, r):
                u, v = n % 2, 1 - n % 2
                if tile_has(t, 2):
                    need(dve, hidT_done, t - 1)
                    need(dve, y_done, t - 3)
                    nc.vector.tensor_copy(hidT[:, u, :], bank[6 + u][:, 0:P]).then_inc(hidT_saved, 1)
                if tile_has(t, 1):
                    need(dve, silu_done, t)
                    need(dve, hidT_done, t - 2)
                    nc.vector.tensor_tensor(hid[:, v, :], bank[4 + v][:, I:2 * I], silu_c[:, v, :],
                                            ALU.mult).then_inc(hid_done, 1)
                if isinstance(t, int) and t == NT + 1:
                    low_of_tokens(1)
                if tile_has(t, 2):
                    need(dve, y_done, t - 1)
                    if isinstance(t, int):
                        need(dve, y_stored[u], 16 * ((t - 2) // 2))
                    else:
                        need(dve, y_stored[u], r * 32 + 16 * ((n - 2) // 2))
                    nc.vector.tensor_copy(y_sb[:, u, :], bank[2 + u][:, :]).then_inc(y_saved, 1)

            tile_steps(dve, tile_step)

            def add_routed(m, n):
                b = (m - 1) * (B // 2) + n
                need(dve, y_fetched[n], m * (16 * TOPK))
                need(dve, x1s_done, m * TM)
                for k, added in enumerate((added1, added2)):
                    if k:
                        need(dve, added1, b + 1)
                    nc.vector.scalar_tensor_tensor(x_at(b), y_back[:, n, k, :], weight[:, k, bass.ds(b, 1)], x_at(b),
                                                   ALU.mult, ALU.add).then_inc(added, 1)

            def low_of_hidden(m, ic):
                need(dve, hidT_high, (m - 1) * IC + ic + 1)
                need(dve, down_s_done, m * IC + ic - 1)
                nc.vector.tensor_tensor(hidT_parts[:, ic % 2, 1, :], hidT_s[:, ic, :],
                                        hidT_parts[:, ic % 2, 0, :].bitcast(F32), ALU.subtract).then_inc(hidT_low, 1)

            low_of_weights(SPLIT_ORDER[0])
            low_of_weights(SPLIT_ORDER[1])
            for n in range(2):
                dve.wait_ge(y_stored[n], 16 * ((NT + 1 - n) // 2))

            for m in range(1, NM):
                for ic in range(IC):
                    hidden_shared(m, ic)
                    low_of_hidden(m, ic)
                    if m == 1 and ic < IC - 2:
                        low_of_weights(SPLIT_ORDER[ic + 2])
                    if m < 3 and ic < IC - 1:
                        add_routed(m, ic * 2)
                        add_routed(m, ic * 2 + 1)
                if m < NM - 1:
                    low_of_tokens(m + 1)
                if m < 3:
                    add_routed(m, B // 2 - 2)
                    add_routed(m, B // 2 - 1)
                need(dve, added2, min(m * (B // 2), B))
                add_shared(m)


def kernel(x, ctx_512, g_xattn, g_ffn, L0_xattn_Wc, L0_xattn_bc, L0_ffn_gate_w, L0_ffn_w1, L0_ffn_w2, L0_ffn_w3,
           L0_ffn_ws_gate, L0_ffn_ws_up, L0_ffn_ws_down, L0_ffn_shared_gate_w):
    import numpy as np
    import concourse.bacc as bacc
    from concourse.bass_utils import run_bass_kernel_spmd

    def parts(w):
        e, n, h = w.shape
        return np.asarray(w).reshape(e, n, h // P, P).transpose(3, 0, 2, 1)

    arrays = {
        "x": np.asarray(x).reshape(B * P, D),
        "ctx": np.asarray(ctx_512).reshape(B * P, NG * HD),
        "keys_t": np.asarray(ctx_512).reshape(B, P, NG, HD).transpose(0, 3, 2, 1).reshape(B * HD, NG * P),
        "g_xattn": np.asarray(g_xattn),
        "g_ffn": np.asarray(g_ffn),
        "wc_t": np.asarray(L0_xattn_Wc).T.reshape(NG, HG, HD, D).transpose(1, 0, 2, 3).reshape(D, D),
        "bc": np.asarray(L0_xattn_bc),
        "gate_t": np.asarray(L0_ffn_gate_w).T,
        "sgate_t": np.asarray(L0_ffn_shared_gate_w).T,
        "w13_t": np.concatenate([parts(L0_ffn_w1), parts(L0_ffn_w3)], axis=3).reshape(P, -1),
        "w2_t": np.asarray(L0_ffn_w2).transpose(2, 0, 1).reshape(P, -1),
        "wsg_t": np.asarray(L0_ffn_ws_gate).T,
        "wsu_t": np.asarray(L0_ffn_ws_up).T,
        "wsd_t": np.asarray(L0_ffn_ws_down).T,
    }
    nc = bacc.Bacc("TRN2", target_bir_lowering=False, num_devices=1)
    ins = {}
    for name in arrays:
        arrays[name] = np.ascontiguousarray(arrays[name])
        ins[name] = nc.dram_tensor(name, arrays[name].shape, mybir.dt.from_np(arrays[name].dtype), kind="ExternalInput").ap()
    xn_dram = nc.dram_tensor("xn_dram", [B * P, D], F32, kind="Internal").ap()
    y_dram = nc.dram_tensor("y_dram", [NT * P, D], F32, kind="Internal").ap()
    out = nc.dram_tensor("out", [B * P, D], F32, kind="ExternalOutput").ap()
    flamingo_block(nc, *ins.values(), xn_dram, y_dram, out)
    r = run_bass_kernel_spmd(nc, [arrays], core_ids=[0])
    return r.results[0]["out"].reshape(B, P, D)
```
